# Optimizing a Trainium2 kernel written in Bass

```python
import numpy as np
import jax
import jax.numpy as jnp

def _softmax(x, axis=-1):
    return jax.nn.softmax(x, axis=axis)

def _gelu(x):
    return jax.nn.gelu(x, approximate=True)

def _silu(x):
    return jax.nn.silu(x)

def _sigmoid(x):
    return jax.nn.sigmoid(x)

def _layernorm(x, axis=-1, eps=1e-05):
    m = jnp.mean(x, axis=axis, keepdims=True)
    v = jnp.var(x, axis=axis, keepdims=True)
    return (x - m) / jnp.sqrt(v + eps)

def _scatter_add(tgt, idx, src, axis=0):
    return tgt.at[idx].add(src)

def _segment_sum(src, seg, n):
    return jax.ops.segment_sum(src, seg, n)
kernel_name = 'mk_xattn_ffn_d1_seqx_r4_223420'

def setup_inputs(seed: int=0):
    np.random.seed(seed)
    _w = jnp.asarray

    def _rec_inputs():
        import jax
        import jax.numpy as jnp
        _rk = jax.random.key(seed)
        x = -0.000125 + 0.9999 * jax.random.normal(jax.random.fold_in(_rk, 1), (16, 128, 512), jnp.float32)
        _lenS = 128 - jax.random.randint(jax.random.fold_in(_rk, 7), (16,), 0, max(1, 128 // 4) + 1, jnp.int32)
        _lenS2 = 128 - jax.random.randint(jax.random.fold_in(_rk, 8), (16,), 0, max(1, 128 // 4) + 1, jnp.int32)
        _ctx_2048P = jax.random.normal(jax.random.fold_in(_rk, 11), (16, 16, 512), jnp.float32)
        _ctx_2048c = jax.random.dirichlet(jax.random.fold_in(_rk, 511), 0.3 * jnp.ones((16,), jnp.float32), (16, 128))
        _ctx_2048t = jnp.einsum('bsk,bkd->bsd', _ctx_2048c, _ctx_2048P)
        _ctx_2048t = _ctx_2048t * jax.lax.rsqrt(jnp.mean(jnp.square(_ctx_2048t)) + 1e-12) * 0.953939
        ctx_2048 = -0.000514642 + 1.00011 * (_ctx_2048t + 0.3 * jax.random.normal(jax.random.fold_in(_rk, 611), (16, 128, 512), jnp.float32))
        _validS = jnp.arange(128)[None, :] < _lenS[:, None]
        _validS2 = jnp.arange(128)[None, :] < _lenS2[:, None]
        _causal = jnp.tril(jnp.ones((128, 128), dtype=bool))
        mask_BxS2_bk0 = jnp.logical_not(jnp.broadcast_to(_validS2[:, :], (16, 128)))
        return (x, ctx_2048, mask_BxS2_bk0)
    x, ctx_2048, mask_BxS2_bk0 = _rec_inputs()

    def _L0_xattn_setup():
        import jax, jax.numpy as jnp
        import numpy as np
        key = jax.random.key(seed)
        k1, k2, k3 = jax.random.split(key, 3)
        B, S, D, M = (8, 512, 512, 128)
        hidden_states = jax.random.normal(k1, (B, S, D), dtype=jnp.float32)
        memory_tokens = jax.random.normal(k2, (B, M, D), dtype=jnp.float32)
        memory_mask = jax.random.randint(k3, (B, M), 0, 2).astype(jnp.bool_)
        return {'hidden_states': hidden_states, 'memory_tokens': memory_tokens, 'memory_mask': memory_mask}
    _L0_xattn_all = _L0_xattn_setup()
    _L0_xattn_in = {k: v for k, v in _L0_xattn_all.items() if k in ()}
    del _L0_xattn_all

    def _L0_ffn_setup():
        import jax, jax.numpy as jnp
        import numpy as np
        B, T = (1, 128)
        DIM = 512
        MOE_INTER = 352
        N_EXPERTS = 64
        TOPK = 6
        N_SHARED = 2
        SHARED_INTER = N_SHARED * MOE_INTER
        CAPACITY = 128
        ROUTE_SCALE = 1.0
        key = jax.random.key(seed)
        ks = jax.random.split(key, 8)

        def w(k, shape, fan_in):
            return jax.random.normal(k, shape, jnp.float32) * fan_in ** (-0.5)
        return {'x': jax.random.normal(ks[0], (B, T, DIM), jnp.float32), 'gate_w': w(ks[1], (N_EXPERTS, DIM), DIM), 'w1': w(ks[2], (N_EXPERTS, MOE_INTER, DIM), DIM), 'w2': w(ks[3], (N_EXPERTS, DIM, MOE_INTER), MOE_INTER), 'w3': w(ks[4], (N_EXPERTS, MOE_INTER, DIM), DIM), 'sw1': w(ks[5], (SHARED_INTER, DIM), DIM), 'sw2': w(ks[6], (DIM, SHARED_INTER), SHARED_INTER), 'sw3': w(ks[7], (SHARED_INTER, DIM), DIM)}
    _L0_ffn_all = _L0_ffn_setup()
    _L0_ffn_in = {k: v for k, v in _L0_ffn_all.items() if k in ('gate_w', 'w1', 'w2', 'w3', 'sw1', 'sw2', 'sw3')}
    del _L0_ffn_all
    return {'x': x, 'ctx_2048': ctx_2048, 'mask_BxS2_bk0': mask_BxS2_bk0, 'L0_ffn_gate_w': _L0_ffn_in['gate_w'], 'L0_ffn_w1': _L0_ffn_in['w1'], 'L0_ffn_w2': _L0_ffn_in['w2'], 'L0_ffn_w3': _L0_ffn_in['w3'], 'L0_ffn_sw1': _L0_ffn_in['sw1'], 'L0_ffn_sw2': _L0_ffn_in['sw2'], 'L0_ffn_sw3': _L0_ffn_in['sw3']}

def reference(x, ctx_2048, mask_BxS2_bk0, L0_ffn_gate_w, L0_ffn_w1, L0_ffn_w2, L0_ffn_w3, L0_ffn_sw1, L0_ffn_sw2, L0_ffn_sw3):
    import jax
    import jax.numpy as jnp

    def _L0_xattn_ref(hidden_states, memory_tokens, memory_mask):
        import jax, jax.numpy as jnp
        import numpy as np
        B, S, D = hidden_states.shape
        scale = 1.0 / jnp.sqrt(jnp.asarray(D, hidden_states.dtype))
        scores = jnp.einsum('bsd,bmd->bsm', hidden_states, memory_tokens) * scale
        neg_inf = jnp.asarray(-1e+30, scores.dtype)
        scores = jnp.where(memory_mask[:, None, :], scores, neg_inf)
        attn = jax.nn.softmax(scores, axis=-1)
        readout = jnp.einsum('bsm,bmd->bsd', attn, memory_tokens)
        valid_b = jnp.any(memory_mask, axis=-1)
        out = jnp.where(valid_b[:, None, None], readout, jnp.zeros_like(readout))
        return out

    def _L0_ffn_ref(x, gate_w, w1, w2, w3, sw1, sw2, sw3):
        import jax, jax.numpy as jnp
        import numpy as np
        B, T = (1, 128)
        DIM = 512
        MOE_INTER = 352
        N_EXPERTS = 64
        TOPK = 6
        N_SHARED = 2
        SHARED_INTER = N_SHARED * MOE_INTER
        CAPACITY = 128
        ROUTE_SCALE = 1.0
        Bb, Tt, D = x.shape
        xf = x.reshape(-1, D)
        N = xf.shape[0]
        logits = xf @ gate_w.T
        scores = jax.nn.softmax(logits, axis=-1)
        gate_vals, idx = jax.lax.top_k(scores, TOPK)
        gate_vals = gate_vals * ROUTE_SCALE
        E = gate_w.shape[0]
        fe = idx.reshape(-1)
        ft = jnp.repeat(jnp.arange(N), TOPK)
        onehot = (fe[:, None] == jnp.arange(E)[None, :]).astype(jnp.int32)
        pos = jnp.take_along_axis(jnp.cumsum(onehot, axis=0) - 1, fe[:, None], axis=1)[:, 0]
        keep = pos < CAPACITY
        buf = jnp.full((E, CAPACITY), N, dtype=jnp.int32)
        buf = buf.at[fe, pos].set(ft.astype(jnp.int32), mode='drop')
        xpad = jnp.concatenate([xf, jnp.zeros((1, D), xf.dtype)], axis=0)
        xe = xpad[buf]
        h = jax.nn.silu(jnp.einsum('ecd,eid->eci', xe, w1)) * jnp.einsum('ecd,eid->eci', xe, w3)
        ye = jnp.einsum('eci,edi->ecd', h, w2)
        pc = jnp.minimum(pos, CAPACITY - 1)
        op = ye[fe, pc] * keep[:, None].astype(ye.dtype)
        routed = (op * gate_vals.reshape(-1)[:, None]).reshape(N, TOPK, D).sum(axis=1)
        z = jax.nn.silu(xf @ sw1.T) * (xf @ sw3.T) @ sw2.T
        return (routed + z).reshape(Bb, Tt, D)
    x = x + _L0_xattn_ref(_layernorm(x, axis=-1), ctx_2048, mask_BxS2_bk0)
    x = x + _L0_ffn_ref(_layernorm(x, axis=-1), L0_ffn_gate_w, L0_ffn_w1, L0_ffn_w2, L0_ffn_w3, L0_ffn_sw1, L0_ffn_sw2, L0_ffn_sw3)
    return x

_drawn_inputs = setup_inputs


def setup_inputs(seed=0):
    import zlib

    import numpy as np

    out = dict(_drawn_inputs(seed))
    spreads = {}
    factors = {}
    for name, (base, spread) in spreads.items():
        noise = np.random.default_rng([zlib.crc32(name.encode()), seed]).standard_normal(out[name].shape)
        drawn = base * np.exp(spread * noise) if base else spread * noise
        out[name] = jnp.asarray(drawn.astype(out[name].dtype))
    for name, factor in factors.items():
        out[name] = (out[name] * factor).astype(out[name].dtype)
    return out
```

```python
import concourse.bass as bass
from concourse import mybir
from contextlib import ExitStack


def cross_attention_moe_kernel(
    nc: bass.Bass,
    x: bass.AP,
    ctx: bass.AP,
    ctx_t: bass.AP,
    mask: bass.AP,
    gate_t: bass.AP,
    w13: bass.AP,
    w2ab: bass.AP,
    w2c: bass.AP,
    out: bass.AP,
):
    F32 = mybir.dt.float32
    F32R = mybir.dt.float32r
    BF16 = mybir.dt.bfloat16
    I32 = mybir.dt.int32
    U32 = mybir.dt.uint32
    U8 = mybir.dt.uint8
    ALU = mybir.AluOpType
    ACT = mybir.ActivationFunctionType
    AX = mybir.AxisListType

    P = 128
    B, S, D = x.shape
    M = ctx.shape[1]
    E = gate_t.shape[2]
    UNITS = w13.shape[0]
    I = w13.shape[3] // 2
    KD = D // P
    SHARED = UNITS - E
    K = 6
    CAP = 128
    N = B * S
    SCALE = float(D) ** -0.5
    EPS = 1e-5
    BIG = 1e30
    HUGE = 3.0e38
    IC = [(0, P), (P, P), (2 * P, I - 2 * P)]
    RAW = 4
    assert S == P and M == P and CAP == P and SHARED == 2 and B % 2 == 0 and E % 4 == 0

    es = ExitStack()
    with es:
        def sb(name, shape, dt=F32):
            return es.enter_context(nc.sbuf_tensor(name, shape, dt))

        def bank(name):
            return es.enter_context(nc.psum_tensor(name, [P, 512], F32))

        def sem(name):
            return es.enter_context(nc.semaphore(name))

        tokens = nc.dram_tensor("tokens", [N + CAP, D], F32, kind="Internal").ap()
        total = nc.dram_tensor("total", [N + CAP, D], F32, kind="Internal").ap()
        table = nc.dram_tensor("slot_table", [CAP * E, 2], I32, kind="Internal").ap()

        raw13 = [sb(f"raw13_{r}", [P, KD * 2 * I]) for r in range(RAW)]
        raw2 = [sb(f"raw2_{r}", [P, 3 * D]) for r in range(RAW)]
        w13h = [sb(f"w13h_{r}", [P, KD * 2 * I], F32R) for r in range(2)]
        w13l = [sb(f"w13l_{r}", [P, KD * 2 * I], F32R) for r in range(2)]
        w2h = [sb(f"w2h_{r}", [P, 3 * D], F32R) for r in range(2)]
        w2l = [sb(f"w2l_{r}", [P, 3 * D], F32R) for r in range(2)]

        ident = sb("ident", [P, P])
        before = sb("before", [P, P], BF16)
        notbefore = sb("notbefore", [P, P], BF16)
        zeros = sb("zeros", [P, D])
        zbf = sb("zbf", [P, P], BF16)
        maskb = sb("maskb", [P, B * M], U8)
        maskf = sb("maskf", [P, B, M])
        maskn = sb("maskn", [P, M])
        valid = sb("valid", [P, B])
        mhalf = sb("mhalf", [P, 1])
        eio_i = sb("eio_i", [P, E], I32)
        eio = sb("eio", [P, E])
        ids = sb("ids", [P, B], I32)
        dflt = sb("dflt", [P, E, 2], I32)
        graw = sb("graw", [P, KD * E])
        gh = sb("gh", [P, KD * E], F32R)
        gl = sb("gl", [P, KD * E], F32R)

        x_in = [sb(f"x_in{p}", [P, D]) for p in range(2)]
        c_in = [sb(f"c_in{p}", [P, D]) for p in range(2)]
        ct_in = [sb(f"ct_in{p}", [P, D]) for p in range(2)]
        xn = sb("xn", [P, D])
        xnT = sb("xnT", [P, D])
        st1 = sb("st1", [P, 6])
        ag1 = sb("ag1", [P, 2])
        ve1 = sb("ve1", [P, 1])
        rs1 = sb("rs1", [P, 1])
        sm = sb("sm", [P, M])
        sn = sb("sn", [P, M])
        smin = sb("smin", [P, 1])
        pr = sb("pr", [P, M])
        rsum = sb("rsum", [P, 1])
        rinv = sb("rinv", [P, 1])
        rval = sb("rval", [P, 1])
        pT = sb("pT", [P, P])
        x2 = [sb(f"x2_{p}", [P, D]) for p in range(2)]
        x2n = [sb(f"x2n_{p}", [P, D]) for p in range(2)]
        st2 = sb("st2", [P, 6])
        ag2 = sb("ag2", [P, 2])
        ve2 = sb("ve2", [P, 1])
        rs2 = sb("rs2", [P, 1])

        top8 = sb("top8", [P, 8])
        idx8 = sb("idx8", [P, 8], U32)
        ntop = sb("ntop", [P, 1])
        etop = sb("etop", [P, 8])
        elog = sb("elog", [P, E])
        esum = sb("esum", [P, 1])
        einv = sb("einv", [P, 1])
        oh = sb("oh", [P, K, E], BF16)
        posx = sb("posx", [P, E])
        ohp = sb("ohp", [P, K, E])
        slot = [sb(f"slot{p}", [P, K], I32) for p in range(2)]
        vals = [sb(f"vals{p}", [P, K, 2], I32) for p in range(2)]

        tTh = sb("tTh", [P, D], F32R)
        tTl = sb("tTl", [P, D], F32R)
        act = sb("act", [P, I])
        gated = sb("gated", [P, I])
        h = sb("h", [P, I])
        hTh = sb("hTh", [P, 3 * P], F32R)
        hTl = sb("hTl", [P, 3 * P], F32R)
        xe = x_in
        y = [sb(f"y{p}", [P, D]) for p in range(2)]
        tabs = sb("tabs", [P, E, 2], I32)
        idx4 = sb("idx4", [P, 4], I32)
        gate4 = sb("gate4", [P, 4])

        UP = [[bank(f"up1_{p}"), bank(f"up3_{p}")] for p in range(2)]
        HT = bank("hT_ps")
        YB = bank("y_ps")
        TB = bank("tT_ps")
        LAST = bank("last_ps")
        RO = UP[1][0]
        MI = UP[1][1]
        POS = LAST

        const_step = sem("const_step")
        const_ready = sem("const_ready")
        mask_in = sem("mask_in")
        gate_in = sem("gate_in")
        mask_ready = sem("mask_ready")
        gateh_ready = sem("gateh_ready")
        gatel_ready = sem("gatel_ready")
        x_ld = [sem(f"x_ld{p}") for p in range(2)]
        c_ld = [sem(f"c_ld{p}") for p in range(2)]
        raw13_in = [sem(f"raw13_in{r}") for r in range(RAW)]
        raw2_in = [sem(f"raw2_in{r}") for r in range(RAW)]
        wh13 = sem("wh13")
        wl13 = sem("wl13")
        wh2 = sem("wh2")
        wl2 = sem("wl2")
        ln1_link = sem("ln1_link")
        var1_ready = sem("var1_ready")
        rstd1_ready = sem("rstd1_ready")
        xn_ready = sem("xn_ready")
        xnT_done = sem("xnT_done")
        xnT_ready = sem("xnT_ready")
        scores_done = sem("scores_done")
        soft_link = sem("soft_link")
        soft_ready = sem("soft_ready")
        probs_ready = sem("probs_ready")
        pT_done = sem("pT_done")
        pT_ready = sem("pT_ready")
        read_done = sem("read_done")
        x2_ready = sem("x2_ready")
        ln2_link = sem("ln2_link")
        var2_ready = sem("var2_ready")
        rstd2_ready = sem("rstd2_ready")
        x2n_ready = sem("x2n_ready")
        tT_done = sem("tT_done")
        tTh_ready = sem("tTh_ready")
        tTl_ready = sem("tTl_ready")
        logits_done = sem("logits_done")
        top_link = sem("top_link")
        top_ready = sem("top_ready")
        etop_ready = sem("etop_ready")
        oh_ready = sem("oh_ready")
        pos_done = sem("pos_done")
        pos_read = sem("pos_read")
        slot_link = sem("slot_link")
        vals_ready = sem("vals_ready")
        table_init = sem("table_init")
        rows_init = sem("rows_init")
        table_st = [sem(f"table_st{p}") for p in range(2)]
        up_done = sem("up_done")
        tanh_ready = sem("tanh_ready")
        gated_link = sem("gated_link")
        h_ready = sem("h_ready")
        hT_done = sem("hT_done")
        hTh_ready = sem("hTh_ready")
        hTl_ready = sem("hTl_ready")
        down_done = sem("down_done")
        sum_ready = sem("sum_ready")
        tok_st = [sem(f"tok_st{p}") for p in range(2)]
        sum_st = [sem(f"sum_st{p}") for p in range(2)]
        table_in = sem("table_in")
        bidx_ready = sem("bidx_ready")
        xe_in = [sem(f"xe_in{p}") for p in range(2)]
        bxT_done = sem("bxT_done")
        bxTh_ready = sem("bxTh_ready")
        bxTl_ready = sem("bxTl_ready")
        bup_done = sem("bup_done")
        bsilu_ready = sem("bsilu_ready")
        bh_ready = sem("bh_ready")
        bhT_done = sem("bhT_done")
        bhTh_ready = sem("bhTh_ready")
        bhTl_ready = sem("bhTl_ready")
        bdown_done = sem("bdown_done")
        by_ready = sem("by_ready")
        added = sem("added")
        out_st = sem("out_st")

        block = es.enter_context(nc.Block())

        def even_odd(eng, first, pairs, step):
            with eng.Fori(0, pairs) as g:
                for j in range(2):
                    step(g * 2 + (first + j), (first + j) % 2, g + (first + j) // 2)

        def by_four(eng, first, fours, step):
            with eng.Fori(first // 4, first // 4 + fours) as g:
                for j in range(4):
                    step(g * 4 + j, j, g)

        def settled(eng):
            eng.nop(nofuse=True)

        @block.sync
        def _(sp):
            def load_chunk(c, p):
                sp.dma_start(x_in[p][:, :], x[c]).then_inc(x_ld[p], 16)
                sp.dma_start(ct_in[p][:, :].rearrange("p (k m) -> p k m", k=KD), ctx_t[c]).then_inc(c_ld[p], 16)
                sp.dma_start(c_in[p][:, :], ctx[c]).then_inc(c_ld[p], 16)

            def load_unit13(w, r):
                sp.dma_start(raw13[r][:, :].rearrange("p (k i) -> p k i", k=KD), w13[w]).then_inc(raw13_in[r], 16)

            def load_unit2(w, r):
                sp.dma_start(raw2[r][:, 0:2 * D].rearrange("p (c n) -> p c n", c=2), w2ab[w]).then_inc(raw2_in[r], 16)
                sp.dma_start(raw2[r][0:IC[2][1], 2 * D:3 * D], w2c[w]).then_inc(raw2_in[r], 16)

            def reload_unit(w, r):
                sp.wait_ge(wl13, w * 2 - 6)
                load_unit13(w, r)
                sp.wait_ge(wl2, w * 2 - 6)
                load_unit2(w, r)

            def step(c, p, half, load=True, attend=True, shared=True):
                if attend:
                    sp.wait_ge(x2n_ready, c + 1)
                    sp.dma_start(tokens[bass.ds(c * P, P), :], x2n[p][:, :]).then_inc(tok_st[p], 16)
                if load:
                    load_chunk(c + 2, p)
                if shared:
                    sp.wait_ge(sum_ready, c)
                    sp.dma_start(total[bass.ds((c - 1) * P, P), :], y[1 - p][:, :]).then_inc(sum_st[1 - p], 16)

            load_chunk(0, 0)
            sp.dma_start(maskb[:, :], mask.rearrange("b m -> (b m)").partition_broadcast(P)).then_inc(mask_in, 16)
            sp.dma_start(graw[:, :].rearrange("p (k e) -> p k e", k=KD), gate_t).then_inc(gate_in, 16)
            load_chunk(1, 1)
            for w in range(RAW):
                load_unit13(w, w)
                load_unit2(w, w)
            step(0, 0, 0, shared=False)
            step(1, 1, 0)
            reload_unit(4, 0)
            reload_unit(5, 1)
            even_odd(sp, 2, (B - 4) // 2, step)
            step(B - 2, 0, B // 2 - 1, load=False)
            step(B - 1, 1, B // 2 - 1, load=False)
            step(B, 0, B // 2, load=False, attend=False)
            with sp.Fori(0, (UNITS - 6) // 4) as g:
                for j in range(4):
                    reload_unit(g * 4 + (6 + j), (6 + j) % 4)
            assert (UNITS - 6) % 4 == 0
            sp.wait_ge(added, 16 * E)
            sp.dma_start(out.rearrange("b s d -> (b s) d"), total[0:N, :]).then_inc(out_st, 16)
            sp.wait_ge(out_st, 16)

        @block.gpsimd
        def _(pool):
            n = [0]

            def made(ins):
                n[0] += 1
                ins.then_inc(const_step, 1)

            made(pool.memset(ident[:, :], 0.0))
            made(pool.memset(before[:, :], 1.0))
            made(pool.memset(notbefore[:, :], 1.0))
            made(pool.memset(zeros[:, :], 0.0))
            made(pool.memset(zbf[:, :], 0.0))
            made(pool.memset(mhalf[:, :], -0.5))
            made(pool.memset(dflt[:, :, :], 0))
            made(pool.iota(eio_i[:, :], pattern=[[1, E]], base=0, channel_multiplier=0))
            made(pool.iota(ids[:, :], pattern=[[P, B]], base=0, channel_multiplier=1))
            pool.wait_ge(const_step, n[0])
            made(pool.affine_select(out=ident[:, :], in_=ident[:, :], compare_op=ALU.not_equal, fill=1.0,
                                    base=0, pattern=[[-1, P]], channel_multiplier=1))
            made(pool.affine_select(out=before[:, :], in_=before[:, :], compare_op=ALU.is_gt, fill=0.0,
                                    base=0, pattern=[[1, P]], channel_multiplier=-1))
            made(pool.affine_select(out=notbefore[:, :], in_=notbefore[:, :], compare_op=ALU.is_ge, fill=0.0,
                                    base=0, pattern=[[-1, P]], channel_multiplier=1))
            made(pool.iota(dflt[:, :, 0], pattern=[[0, E]], base=N, channel_multiplier=1))
            pool.wait_ge(const_step, n[0])
            pool.sem_inc(const_ready, 1)
            pool.dma_start(table.rearrange("(p e) two -> p (e two)", p=P),
                           dflt[:, :, :].rearrange("p e two -> p (e two)")).then_inc(table_init, 16)
            pool.dma_start(tokens[N:N + CAP, :], zeros[:, :]).then_inc(rows_init, 16)
            pool.dma_start(total[N:N + CAP, :], zeros[:, :]).then_inc(rows_init, 16)

            def rstd(c, var_ready, ve, rs, ready):
                pool.wait_ge(var_ready, c + 1)
                pool.tensor_tensor(rs[:, :], ve[:, :], mhalf[:, :], ALU.pow).then_inc(ready, 1)

            def step(c, p, half, attend=True, shared=True, ahead=True):
                if shared:
                    pool.wait_ge(vals_ready, c)
                    settled(pool)
                    for k in range(K):
                        pool.indirect_dma_start(
                            out=table[:, :], out_offset=bass.IndirectOffsetOnAxis(ap=slot[1 - p][:, k:k + 1], axis=0),
                            in_=vals[1 - p][:, k, :], in_offset=None,
                            bounds_check=CAP * E - 1, oob_is_err=False).then_inc(table_st[1 - p], 16)
                if attend:
                    rstd(c, var2_ready, ve2, rs2, rstd2_ready)
                if ahead:
                    rstd(c + 1, var1_ready, ve1, rs1, rstd1_ready)

            rstd(0, var1_ready, ve1, rs1, rstd1_ready)
            pool.wait_ge(table_init, 16)
            step(0, 0, 0, shared=False)
            even_odd(pool, 1, (B - 2) // 2, step)
            step(B - 1, 1, B // 2 - 1, ahead=False)
            step(B, 0, B // 2, attend=False, ahead=False)

            for p in range(2):
                pool.wait_ge(table_st[p], 16 * K * B // 2)
            pool.dma_start(tabs[:, :, :].rearrange("p e two -> p (e two)"),
                           table.rearrange("(p e) two -> p (e two)", p=P)).then_inc(table_in, 16)
            pool.wait_ge(rows_init, 32)
            for p in range(2):
                pool.wait_ge(tok_st[p], 16 * B // 2)
                pool.wait_ge(sum_st[p], 16 * B // 2)

            def gather(e, q):
                pool.wait_ge(bidx_ready, e + 1)
                settled(pool)
                pool.indirect_dma_start(
                    out=xe[q % 2][:, :], out_offset=None, in_=tokens[:, :],
                    in_offset=bass.IndirectOffsetOnAxis(ap=idx4[:, q:q + 1], axis=0),
                    bounds_check=N + CAP - 1, oob_is_err=True).then_inc(xe_in[q % 2], 16)

            def scatter(e, q, first=False):
                pool.wait_ge(by_ready, e + 1)
                if not first:
                    pool.wait_ge(added, e * 16)
                settled(pool)
                pool.indirect_dma_start(
                    out=total[:, :], out_offset=bass.IndirectOffsetOnAxis(ap=idx4[:, q:q + 1], axis=0),
                    in_=y[q % 2][:, :], in_offset=None,
                    bounds_check=N + CAP - 1, oob_is_err=True, compute_op=ALU.add).then_inc(added, 16)

            gather(0, 0)
            gather(1, 1)

            def expert(e, q, g=None, ahead=True, behind=True, first=False):
                if ahead:
                    pool.wait_ge(bxT_done, e + 1)
                    gather(e + 2, (q + 2) % 4)
                if behind:
                    scatter(e - 1, (q - 1) % 4, first=first)

            expert(0, 0, behind=False)
            expert(1, 1, first=True)
            expert(2, 2)
            expert(3, 3)
            by_four(pool, 4, E // 4 - 2, expert)
            for e in range(E - 4, E):
                expert(e, e % 4, ahead=e + 2 < E)
            scatter(E - 1, (E - 1) % 4)
            pool.wait_ge(added, 16 * E)

        @block.scalar
        def _(ac):
            def split13(w, r, q, use, free):
                ac.wait_ge(raw13_in[r], use * 16 + 16)
                free()
                n = KD * I
                for a in range(2):
                    ac.activation(w13h[q][:, a * n:(a + 1) * n], raw13[r][:, a * n:(a + 1) * n],
                                  ACT.Copy).then_inc(wh13, 1)

            def split2(w, r, q, use, free):
                ac.wait_ge(raw2_in[r], use * 32 + 32)
                free()
                ac.activation(w2h[q][:, 0:2 * D], raw2[r][:, 0:2 * D], ACT.Copy).then_inc(wh2, 1)
                ac.activation(w2h[q][0:IC[2][1], 2 * D:3 * D], raw2[r][0:IC[2][1], 2 * D:3 * D],
                              ACT.Copy).then_inc(wh2, 1)

            def hi_of_hT(done, at, freed, free_at, ready):
                ac.wait_ge(done, at)
                if free_at is not None:
                    ac.wait_ge(freed, free_at)
                ac.activation(hTh[:, 0:2 * P], HT[:, 0:2 * P], ACT.Copy)
                ac.activation(hTh[0:IC[2][1], 2 * P:3 * P], HT[0:IC[2][1], 2 * P:3 * P], ACT.Copy).then_inc(ready, 1)

            def shared_half(s, u, first):
                ac.wait_ge(up_done, s * 2 + (u + 1))
                if not (first and u == 0):
                    ac.wait_ge(h_ready, s * 2 + u)
                ac.activation(act[:, :], UP[0][0][:, 0:I], ACT.Tanh, scale=0.5).then_inc(tanh_ready, 1)

            def shared_hT(s, u, first):
                hi_of_hT(hT_done, s * 2 + (u + 1), down_done, None if first and u == 0 else s * 2 + u, hTh_ready)

            def step(c, p, half, attend=True, shared=True, first=False):
                s = c - 1
                if attend:
                    ac.wait_ge(xnT_done, c + 1)
                    if shared:
                        ac.wait_ge(scores_done, c)
                    ac.activation(xnT[:, :], RO[:, :], ACT.Copy).then_inc(xnT_ready, 1)
                if shared:
                    ac.wait_ge(top_ready, s + 1)
                    ac.activation(elog[:, :], MI[:, 0:E], ACT.Exp, bias=ntop[:, :], accum_out=esum[:, :])
                    ac.activation(etop[:, :], top8[:, :], ACT.Exp, bias=ntop[:, :]).then_inc(etop_ready, 1)
                    shared_half(s, 0, first)
                    shared_hT(s, 0, first)
                if attend:
                    ac.wait_ge(soft_ready, c + 1)
                    if shared:
                        ac.wait_ge(pT_done, c)
                    ac.activation(pr[:, :], sn[:, :], ACT.Exp, bias=smin[:, :], scale=-1.0,
                                  accum_out=rsum[:, :]).then_inc(probs_ready, 1)
                if shared:
                    shared_half(s, 1, first)
                    shared_hT(s, 1, first)
                if attend:
                    ac.wait_ge(tT_done, c + 1)
                    if shared:
                        ac.wait_ge(up_done, c * 2)
                    ac.activation(tTh[:, :], TB[:, :], ACT.Copy).then_inc(tTh_ready, 1)

            ac.wait_ge(gate_in, 16)
            ac.activation(gh[:, :], graw[:, :], ACT.Copy).then_inc(gateh_ready, 1)
            step(0, 0, 0, shared=False, first=True)
            for w in range(SHARED):
                split13(w, w, w, 0, lambda: None)
                split2(w, w, w, 0, lambda: None)
            step(1, 1, 0, first=True)
            step(2, 0, 1)
            even_odd(ac, 3, (B - 4) // 2, step)
            step(B - 1, 1, B // 2 - 1)
            step(B, 0, B // 2, attend=False)

            def silu(e, q, first=False):
                ac.wait_ge(bup_done, e + 1)
                if not first:
                    ac.wait_ge(bh_ready, e)
                ac.activation(act[:, :], UP[q % 2][0][:, 0:I], ACT.Silu).then_inc(bsilu_ready, 1)

            def hi_of_x(e, free):
                ac.wait_ge(bxT_done, e + 1)
                free()
                ac.activation(tTh[:, :], TB[:, :], ACT.Copy).then_inc(bxTh_ready, 1)

            def weigh(e, q, wait_added=True):
                ac.wait_ge(bdown_done, e + 1)
                if wait_added:
                    ac.wait_ge(added, (e - 1) * 16)
                ac.activation(y[q % 2][:, :], YB[:, :], ACT.Copy, scale=gate4[:, q:q + 1]).then_inc(by_ready, 1)

            def expert(e, q, g, ahead=True, behind=True):
                w = e + 2
                if behind:
                    hi_of_hT(bhT_done, e, bdown_done, None if isinstance(e, int) and e == 1 else e - 1, bhTh_ready)
                if ahead:
                    def free13():
                        if isinstance(e, int) and e == 0:
                            ac.wait_ge(up_done, 2 * B)
                        else:
                            ac.wait_ge(bup_done, e)
                    split13(w + 1, (q + 3) % 4, (q + 1) % 2, g + (q + 3) // 4, free13)
                silu(e, q, first=isinstance(e, int) and e == 0)
                if ahead:
                    hi_of_x(e + 1, lambda: ac.wait_ge(bup_done, e + 1))

                def free2():
                    if isinstance(e, int) and e < 2:
                        ac.wait_ge(down_done, 2 * B - 1 + e)
                    else:
                        ac.wait_ge(bdown_done, e - 1)
                split2(w, (q + 2) % 4, q % 2, g + (q + 2) // 4, free2)
                if behind:
                    weigh(e - 1, (q - 1) % 4, wait_added=not (isinstance(e, int) and e < 3))

            split13(2, 2, 0, 0, lambda: ac.wait_ge(up_done, 2 * B - 1))
            hi_of_x(0, lambda: ac.wait_ge(up_done, 2 * B))
            for e in range(4):
                expert(e, e, 0, behind=e > 0)
            by_four(ac, 4, E // 4 - 2, expert)
            for e in range(E - 4, E):
                expert(e, e % 4, e // 4, ahead=e + 1 < E)
            hi_of_hT(bhT_done, E, bdown_done, E - 1, bhTh_ready)
            weigh(E - 1, (E - 1) % 4)

        @block.vector
        def _(ve):
            class Links:

                def __init__(self, s, n, step):
                    self.s, self.n, self.base, self.k = s, n, step * n, 0

                def done(self, ins):
                    ins.then_inc(self.s, 1)
                    self.k += 1
                    assert self.k <= self.n

                def wait(self):
                    ve.wait_ge(self.s, self.base + self.k)

            def split13(r, q, at):
                n = KD * I
                for a in range(2):
                    ve.wait_ge(wh13, at + (a + 1))
                    ve.tensor_tensor(w13l[q][:, a * n:(a + 1) * n], raw13[r][:, a * n:(a + 1) * n],
                                     w13h[q][:, a * n:(a + 1) * n].bitcast(F32), ALU.subtract).then_inc(wl13, 1)

            def split2(r, q, at):
                parts = [(P, 0, 2 * D), (IC[2][1], 2 * D, 3 * D)]
                for a, (rows, lo, hi) in enumerate(parts):
                    ve.wait_ge(wh2, at + (a + 1))
                    ve.tensor_tensor(w2l[q][0:rows, lo:hi], raw2[r][0:rows, lo:hi],
                                     w2h[q][0:rows, lo:hi].bitcast(F32), ALU.subtract).then_inc(wl2, 1)

            def lo_of_hT(hi_ready, at, ready):
                ve.wait_ge(hi_ready, at)
                ve.tensor_tensor(hTl[:, 0:2 * P], HT[:, 0:2 * P], hTh[:, 0:2 * P].bitcast(F32), ALU.subtract)
                n = IC[2][1]
                ve.tensor_tensor(hTl[0:n, 2 * P:3 * P], HT[0:n, 2 * P:3 * P], hTh[0:n, 2 * P:3 * P].bitcast(F32),
                                 ALU.subtract).then_inc(ready, 1)

            def lo_of_x(hi_ready, at, ready):
                ve.wait_ge(hi_ready, at)
                ve.tensor_tensor(tTl[:, :], TB[:, :], tTh[:, :].bitcast(F32), ALU.subtract).then_inc(ready, 1)

            def norm_stats(c, src, st, ag, vv, link, ready):
                ln = Links(link, 2, c)
                ln.done(ve.bn_stats(st[:, :], src))
                ln.wait()
                settled(ve)
                ln.done(ve.bn_aggr(ag[:, :], st[:, :]))
                ln.wait()
                ve.tensor_scalar(vv[:, :], ag[:, 1:2], EPS, None, ALU.add).then_inc(ready, 1)

            def norm1_stats(c, p, half):
                ve.wait_ge(x_ld[p], half * 16 + 16)
                norm_stats(c, x_in[p][:, :], st1, ag1, ve1, ln1_link, var1_ready)

            def norm1_apply(c, p, first=False):
                ve.wait_ge(rstd1_ready, c + 1)
                if not first:
                    ve.wait_ge(xnT_done, c)
                ve.tensor_scalar(xn[:, :], x_in[p][:, :], ag1[:, 0:1], rs1[:, 0:1], ALU.subtract,
                                 ALU.mult).then_inc(xn_ready, 1)

            def route_top(s):
                ve.wait_ge(logits_done, s + 1)
                settled(ve)
                ln = Links(top_link, 2, s)
                ln.done(ve.max(top8[:, :], MI[:, 0:E]))
                ln.wait()
                settled(ve)
                ln.done(ve.max_index(idx8[:, :], top8[:, :], MI[:, 0:E]))
                ve.tensor_scalar(ntop[:, :], top8[:, 0:1], -1.0, None, ALU.mult).then_inc(top_ready, 1)
                ln.wait()
                ve.tensor_tensor(oh[:, :, :], idx8[:, 0:K].unsqueeze(2).to_broadcast([P, K, E]),
                                 eio[:, :].unsqueeze(1).to_broadcast([P, K, E]), ALU.is_equal).then_inc(oh_ready, 1)

            def route_slots(s, p, half):
                ve.wait_ge(pos_done, s + 1)
                ve.scalar_tensor_tensor(posx[:, :], POS[:, 0:E], float(E), eio[:, :], ALU.mult,
                                        ALU.add).then_inc(pos_read, 1)
                ve.wait_ge(etop_ready, s + 1)
                ln = Links(slot_link, 2, s)
                ln.done(ve.reciprocal(einv[:, :], esum[:, :]))
                if not (isinstance(s, int) and s < 2):
                    ve.wait_ge(table_st[p], half * (16 * K))
                ve.tensor_copy(vals[p][:, :, 0], ids[:, bass.ds(s, 1)].to_broadcast([P, K]))
                ve.wait_ge(pos_read, s + 1)
                ln.done(ve.tensor_tensor(ohp[:, :, :], oh[:, :, :], posx[:, :].unsqueeze(1).to_broadcast([P, K, E]),
                                         ALU.mult))
                ln.wait()
                ve.tensor_scalar(vals[p][:, :, 1].bitcast(F32), etop[:, 0:K], einv[:, 0:1], None, ALU.mult)
                with nc.allow_low_precision(reason="whole numbers under 2 ** 24, one of each row's nonzero"):
                    ve.tensor_reduce(slot[p][:, :], ohp[:, :, :], AX.X, ALU.add).then_inc(vals_ready, 1)

            def shared_gate(s, u):
                ve.wait_ge(tanh_ready, s * 2 + (u + 1))
                ve.scalar_tensor_tensor(gated[:, :], act[:, :], 1.0, UP[0][0][:, 0:I], ALU.add,
                                        ALU.mult).then_inc(gated_link, 1)
                if not (isinstance(s, int) and s == 0 and u == 0):
                    ve.wait_ge(hT_done, s * 2 + u)
                ve.wait_ge(gated_link, s * 2 + (u + 1))
                ve.scalar_tensor_tensor(h[:, :], gated[:, :], 0.5, UP[0][1][:, 0:I], ALU.mult,
                                        ALU.mult).then_inc(h_ready, 1)

            def step(c, p, half, attend=True, shared=True, ahead=True):
                s, ps = c - 1, 1 - p
                halfs = half - 1 + p
                if shared:
                    route_top(s)
                    shared_gate(s, 0)
                    route_slots(s, ps, halfs)
                if attend:
                    ve.tensor_scalar(maskn[:, :], maskf[:, bass.ds(c, 1), :].squeeze(1), -BIG, BIG, ALU.mult, ALU.add)
                    ve.wait_ge(scores_done, c + 1)
                    ve.scalar_tensor_tensor(sm[:, :], MI[:, 0:M], -SCALE, maskf[:, bass.ds(c, 1), :].squeeze(1),
                                            ALU.mult, ALU.mult).then_inc(soft_link, 1)
                    ve.wait_ge(soft_link, c + 1)
                    settled(ve)
                    ve.tensor_tensor_reduce(out=sn[:, :], in0=sm[:, :], in1=maskn[:, :],
                                            scale=1.0, scalar=HUGE, op0=ALU.add, op1=ALU.min,
                                            accum_out=smin[:, :]).then_inc(soft_ready, 1)
                if shared:
                    lo_of_hT(hTh_ready, s * 2 + 1, hTl_ready)
                if attend:
                    ve.wait_ge(probs_ready, c + 1)
                    ve.reciprocal(rinv[:, :], rsum[:, :]).then_inc(ln2_link, 1)
                    ve.wait_ge(pT_done, c + 1)
                    ve.tensor_copy(pT[:, :], MI[:, M:2 * M]).then_inc(pT_ready, 1)
                    ve.wait_ge(ln2_link, c * 4 + 1)
                    ve.tensor_scalar(rval[:, :], rinv[:, :], valid[:, bass.ds(c, 1)], None,
                                     ALU.mult).then_inc(ln2_link, 1)
                if shared:
                    shared_gate(s, 1)
                if attend:
                    ve.wait_ge(read_done, c + 1)
                    ve.wait_ge(ln2_link, c * 4 + 2)
                    ve.scalar_tensor_tensor(x2[p][:, :], RO[:, :], rval[:, :], x_in[p][:, :], ALU.mult,
                                            ALU.add).then_inc(x2_ready, 1)
                    ve.wait_ge(x2_ready, c + 1)
                    ve.bn_stats(st2[:, :], x2[p][:, :]).then_inc(ln2_link, 1)
                    ve.wait_ge(ln2_link, c * 4 + 3)
                    settled(ve)
                    ve.bn_aggr(ag2[:, :], st2[:, :]).then_inc(ln2_link, 1)
                    ve.wait_ge(ln2_link, c * 4 + 4)
                    ve.tensor_scalar(ve2[:, :], ag2[:, 1:2], EPS, None, ALU.add).then_inc(var2_ready, 1)
                if shared:
                    lo_of_hT(hTh_ready, s * 2 + 2, hTl_ready)
                if attend:
                    ve.wait_ge(rstd2_ready, c + 1)
                    if not (isinstance(c, int) and c < 2):
                        ve.wait_ge(tok_st[p], half * 16)
                    ve.tensor_scalar(x2n[p][:, :], x2[p][:, :], ag2[:, 0:1], rs2[:, 0:1], ALU.subtract,
                                     ALU.mult).then_inc(x2n_ready, 1)
                if ahead:
                    norm1_stats(c + 1, 1 - p, half + p)
                if shared:
                    ve.wait_ge(down_done, s * 2 + 2)
                    if not (isinstance(s, int) and s < 2):
                        ve.wait_ge(sum_st[ps], halfs * 16)
                    ve.tensor_tensor(y[ps][:, :], YB[:, :], x2[ps][:, :], ALU.add).then_inc(sum_ready, 1)
                if ahead:
                    norm1_apply(c + 1, 1 - p)
                if attend:
                    lo_of_x(tTh_ready, c + 1, tTl_ready)

            norm1_stats(0, 0, 0)
            norm1_apply(0, 0, first=True)
            ve.wait_ge(mask_in, 16)
            ve.tensor_copy(maskf[:, :, :].rearrange("p b m -> p (b m)"), maskb[:, :]).then_inc(mask_ready, 1)
            ve.wait_ge(mask_ready, 1)
            ve.tensor_reduce(valid[:, :], maskf[:, :, :], AX.X, ALU.max).then_inc(mask_ready, 1)
            ve.wait_ge(const_ready, 1)
            ve.tensor_copy(eio[:, :], eio_i[:, :]).then_inc(mask_ready, 1)
            ve.wait_ge(mask_ready, 3)
            ve.wait_ge(gateh_ready, 1)
            ve.tensor_tensor(gl[:, :], graw[:, :], gh[:, :].bitcast(F32), ALU.subtract).then_inc(gatel_ready, 1)
            step(0, 0, 0, shared=False)
            for w in range(SHARED):
                split13(w, w, 2 * w)
                split2(w, w, 2 * w)
            step(1, 1, 0)
            step(2, 0, 1)
            even_odd(ve, 3, (B - 4) // 2, step)
            step(B - 1, 1, B // 2 - 1, ahead=False)
            step(B, 0, B // 2, attend=False, ahead=False)

            def slots_of(e, q, reuse=True):
                if reuse:
                    ve.wait_ge(added, (e - 3) * 16)
                ve.tensor_copy(gate4[:, q:q + 1], tabs[:, bass.ds(e, 1), 1].bitcast(F32))
                ve.tensor_copy(idx4[:, q:q + 1], tabs[:, bass.ds(e, 1), 0]).then_inc(bidx_ready, 1)

            def gate(e, q, first=False):
                ve.wait_ge(bsilu_ready, e + 1)
                if not first:
                    ve.wait_ge(bhT_done, e)
                ve.tensor_tensor(h[:, :], act[:, :], UP[q % 2][1][:, 0:I], ALU.mult).then_inc(bh_ready, 1)

            def expert(e, q, g=None, ahead=True, behind=True):
                if behind:
                    lo_of_hT(bhTh_ready, e, bhTl_ready)
                if ahead:
                    split13((q + 3) % 4, (q + 1) % 2, (e + 3) * 2)
                gate(e, q, first=isinstance(e, int) and e == 0)
                if ahead:
                    lo_of_x(bxTh_ready, e + 2, bxTl_ready)
                split2((q + 2) % 4, q % 2, (e + 2) * 2)
                if not isinstance(e, int) or e + 2 < E:
                    slots_of(e + 2, (q + 2) % 4, reuse=not (isinstance(e, int) and e < 2))

            split13(2, 0, 4)
            ve.wait_ge(table_in, 16)
            slots_of(0, 0, reuse=False)
            slots_of(1, 1, reuse=False)
            lo_of_x(bxTh_ready, 1, bxTl_ready)
            for e in range(4):
                expert(e, e, behind=e > 0)
            by_four(ve, 4, E // 4 - 2, expert)
            for e in range(E - 4, E):
                expert(e, e % 4, ahead=e + 1 < E)
            lo_of_hT(bhTh_ready, E, bhTl_ready)

        @block.tensor
        def _(pe):
            def transpose4(dst, src):
                for k in range(KD):
                    last = pe.transpose(dst[:, k * P:(k + 1) * P], src[:, k * P:(k + 1) * P], ident[:, :])
                return last

            def transpose_h():
                for j, (lo, n) in enumerate(IC):
                    last = pe.transpose(HT[0:n, j * P:(j + 1) * P], h[:, lo:lo + n], ident[:, :])
                return last

            def up(q, banks, halfway=None):
                for k in range(KD):
                    if k == KD // 2 and halfway:
                        halfway()
                    for a, b in ((tTh, w13h[q]), (tTh, w13l[q]), (tTl, w13h[q])):
                        for v in range(2):
                            o = (2 * k + v) * I
                            last = pe.matmul(banks[v][:, 0:I], a[:, k * P:(k + 1) * P], b[:, o:o + I],
                                             start=(k == 0 and a is tTh and b is w13h[q]),
                                             stop=(k == KD - 1 and a is tTl))
                return last

            def down(q, start=True, stop=True):
                for j, (lo, n) in enumerate(IC):
                    for a, b in ((hTh, w2h[q]), (hTh, w2l[q]), (hTl, w2h[q])):
                        last = pe.matmul(YB[:, :], a[0:n, j * P:(j + 1) * P], b[0:n, j * D:(j + 1) * D],
                                         start=(start and j == 0 and a is hTh and b is w2h[q]),
                                         stop=(stop and j == 2 and a is hTl))
                return last

            def count(sel, first=False):
                for k in range(K):
                    last = pe.matmul(POS[:, 0:E], sel[:, :], oh[:, k, :], start=False, stop=False,
                                     skip_group_check=True)
                return last

            def shared_up(s, u, weights=False):
                if not (isinstance(s, int) and s == 0 and u == 0):
                    pe.wait_ge(h_ready, s * 2 + u)
                if weights:
                    pe.wait_ge(wl13, 2 * u + 1)
                up(u, UP[0], halfway=(lambda: pe.wait_ge(wl13, 2 * u + 2)) if weights else None).then_inc(up_done, 1)

            def shared_hT(s, u):
                pe.wait_ge(h_ready, s * 2 + (u + 1))
                if not (isinstance(s, int) and s == 0 and u == 0):
                    pe.wait_ge(hTl_ready, s * 2 + u)
                transpose_h().then_inc(hT_done, 1)

            def shared_down(s, u, weights=False):
                pe.wait_ge(hTl_ready, s * 2 + (u + 1))
                if u == 0 and not (isinstance(s, int) and s == 0):
                    pe.wait_ge(sum_ready, s)
                if weights:
                    pe.wait_ge(wl2, 2 * u + 2)
                down(u, start=(u == 0), stop=(u == 1)).then_inc(down_done, 1)

            def step(c, p, half, attend=True, shared=True, weights=False):
                s = c - 1
                if attend:
                    pe.wait_ge(xn_ready, c + 1)
                    if shared:
                        pe.wait_ge(x2_ready, c)
                    transpose4(RO, xn).then_inc(xnT_done, 1)
                if shared:
                    pe.wait_ge(tTl_ready, s + 1)
                    for k in range(KD):
                        for a, b in ((tTh, gh), (tTh, gl), (tTl, gh)):
                            last = pe.matmul(MI[:, 0:E], a[:, k * P:(k + 1) * P], b[:, k * E:(k + 1) * E],
                                             start=(k == 0 and a is tTh and b is gh), stop=(k == KD - 1 and a is tTl))
                    last.then_inc(logits_done, 1)
                    shared_up(s, 0, weights)
                    pe.wait_ge(oh_ready, s + 1)
                    count(before).then_inc(pos_done, 1)
                if attend:
                    pe.wait_ge(xnT_ready, c + 1)
                    pe.wait_ge(c_ld[p], half * 32 + 32)
                    if shared:
                        pe.wait_ge(etop_ready, c)
                    for k in range(KD):
                        last = pe.matmul(MI[:, 0:M], xnT[:, k * P:(k + 1) * P], ct_in[p][:, k * M:(k + 1) * M],
                                         start=(k == 0), stop=(k == KD - 1))
                    last.then_inc(scores_done, 1)
                if shared:
                    shared_hT(s, 0)
                    pe.wait_ge(pos_read, s + 1)
                    count(notbefore)
                    shared_up(s, 1, weights)
                if attend:
                    pe.wait_ge(probs_ready, c + 1)
                    pe.transpose(MI[:, M:2 * M], pr[:, :], ident[:, :]).then_inc(pT_done, 1)
                if shared:
                    shared_down(s, 0, weights)
                if attend:
                    pe.wait_ge(pT_ready, c + 1)
                    pe.matmul(RO[:, :], pT[:, :], c_in[p][:, :], start=True, stop=True).then_inc(read_done, 1)
                if shared:
                    shared_hT(s, 1)
                    shared_down(s, 1, weights)
                if attend:
                    pe.wait_ge(x2n_ready, c + 1)
                    transpose4(TB, x2n[p]).then_inc(tT_done, 1)

            pe.wait_ge(const_ready, 1)
            pe.matmul(POS[:, 0:E], zbf[:, :], zbf[:, 0:E], start=True, stop=False, skip_group_check=True)
            step(0, 0, 0, shared=False)
            pe.wait_ge(gatel_ready, 1)
            step(1, 1, 0, weights=True)
            even_odd(pe, 2, (B - 2) // 2, step)
            step(B, 0, B // 2, attend=False)

            def transpose_x(e, q):
                pe.wait_ge(xe_in[q % 2], e)
                transpose4(TB, xe[q % 2]).then_inc(bxT_done, 1)

            def expert(e, q, g, ahead=True, behind=True):
                pe.wait_ge(bxTl_ready, e + 1)
                if not (isinstance(e, int) and e < 2):
                    pe.wait_ge(bh_ready, e - 1)
                pe.wait_ge(wl13, (e + 2) * 2 + 1)
                up(q % 2, UP[q % 2], halfway=lambda: pe.wait_ge(wl13, (e + 2) * 2 + 2)).then_inc(bup_done, 1)
                if ahead:
                    g2 = g * 2 + (q + 1) // 2
                    transpose_x(g2 * 16 + 16, (q + 1) % 4)
                if behind:
                    pe.wait_ge(bhTl_ready, e)
                    pe.wait_ge(wl2, (e + 2) * 2)
                    if not (isinstance(e, int) and e < 2):
                        pe.wait_ge(by_ready, e - 1)
                    down((q - 1) % 2).then_inc(bdown_done, 1)
                pe.wait_ge(bh_ready, e + 1)
                transpose_h().then_inc(bhT_done, 1)

            transpose_x(16, 0)
            for e in range(4):
                expert(e, e, 0, behind=e > 0)
            by_four(pe, 4, E // 4 - 2, expert)
            for e in range(E - 4, E):
                expert(e, e % 4, e // 4, ahead=e + 1 < E)
            pe.wait_ge(bhTl_ready, E)
            pe.wait_ge(wl2, (E + 2) * 2)
            pe.wait_ge(by_ready, E - 1)
            down((E - 1) % 2).then_inc(bdown_done, 1)


def kernel(**inputs):
    import numpy as _np
    import concourse.bacc as _bacc
    from concourse import mybir as _mybir
    from concourse.bass_utils import run_bass_kernel_spmd as _run

    x = _np.ascontiguousarray(inputs["x"])
    ctx = _np.ascontiguousarray(inputs["ctx_2048"])
    mask = _np.ascontiguousarray(inputs["mask_BxS2_bk0"])
    gate_w, w1, w2, w3, sw1, sw2, sw3 = (
        _np.asarray(inputs["L0_ffn_" + n]) for n in ("gate_w", "w1", "w2", "w3", "sw1", "sw2", "sw3"))
    B, S, D = x.shape
    E, I, _ = w1.shape
    kd, n2 = D // 128, sw1.shape[0] // I
    a1 = _np.concatenate([sw1.reshape(n2, I, D), w1])
    a3 = _np.concatenate([sw3.reshape(n2, I, D), w3])
    a2 = _np.concatenate([sw2.reshape(D, n2, I).transpose(1, 0, 2), w2])
    w13 = _np.stack([a1, a3], axis=1).reshape(n2 + E, 2 * I, kd, 128).transpose(0, 3, 2, 1)
    a2 = a2.transpose(0, 2, 1)
    arrays = {
        "x": x,
        "ctx": ctx,
        "ctx_t": ctx.reshape(B, S, kd, 128).transpose(0, 3, 2, 1),
        "mask": mask,
        "gate_t": gate_w.reshape(E, kd, 128).transpose(2, 1, 0),
        "w13": w13,
        "w2ab": a2[:, 0:256].reshape(n2 + E, 2, 128, D).transpose(0, 2, 1, 3),
        "w2c": a2[:, 256:],
    }
    nc = _bacc.Bacc("TRN2", target_bir_lowering=False, num_devices=1)
    args, ins = [], {}
    for name, a in arrays.items():
        a = _np.ascontiguousarray(a)
        ins[f"in_{name}"] = a
        args.append(nc.dram_tensor(f"in_{name}", a.shape, _mybir.dt.from_np(a.dtype), kind="ExternalInput").ap())
    args.append(nc.dram_tensor("out_0", (B, S, D), _mybir.dt.float32, kind="ExternalOutput").ap())
    cross_attention_moe_kernel(nc, *args)
    r = _run(nc, [ins], core_ids=[0])
    return r.results[0]["out_0"]
```

```python
import concourse.bass as bass
from concourse import mybir
from contextlib import ExitStack


def cross_attention_moe_kernel(
    nc: bass.Bass,
    x: bass.AP,
    ctx: bass.AP,
    ctx_t: bass.AP,
    mask: bass.AP,
    gate_t: bass.AP,
    w13: bass.AP,
    w2ab: bass.AP,
    w2c: bass.AP,
    out: bass.AP,
):
    F32 = mybir.dt.float32
    F32R = mybir.dt.float32r
    BF16 = mybir.dt.bfloat16
    I32 = mybir.dt.int32
    U32 = mybir.dt.uint32
    U8 = mybir.dt.uint8
    ALU = mybir.AluOpType
    ACT = mybir.ActivationFunctionType
    AX = mybir.AxisListType

    P = 128
    B, S, D = x.shape
    M = ctx.shape[1]
    E = gate_t.shape[2]
    UNITS = w13.shape[0]
    I = w13.shape[3] // 2
    KD = D // P
    SHARED = UNITS - E
    K = 6
    CAP = 128
    N = B * S
    SCALE = float(D) ** -0.5
    EPS = 1e-5
    BIG = 1e30
    HUGE = 3.0e38
    IC = [(0, P), (P, P), (2 * P, I - 2 * P)]
    RAW = 4
    assert S == P and M == P and CAP == P and SHARED == 2 and B % 2 == 0 and E % 4 == 0

    es = ExitStack()
    with es:
        def sb(name, shape, dt=F32):
            return es.enter_context(nc.sbuf_tensor(name, shape, dt))

        def bank(name):
            return es.enter_context(nc.psum_tensor(name, [P, 512], F32))

        def sem(name):
            return es.enter_context(nc.semaphore(name))

        tokens = nc.dram_tensor("tokens", [N + CAP, D], F32, kind="Internal").ap()
        total = nc.dram_tensor("total", [N + CAP, D], F32, kind="Internal").ap()
        table = nc.dram_tensor("slot_table", [CAP * E, 2], I32, kind="Internal").ap()

        raw13 = [sb(f"raw13_{r}", [P, KD * 2 * I]) for r in range(RAW)]
        raw2 = [sb(f"raw2_{r}", [P, 3 * D]) for r in range(RAW)]
        w13h = [sb(f"w13h_{r}", [P, KD * 2 * I], F32R) for r in range(2)]
        w13l = [sb(f"w13l_{r}", [P, KD * 2 * I], F32R) for r in range(2)]
        w2h = [sb(f"w2h_{r}", [P, 3 * D], F32R) for r in range(2)]
        w2l = [sb(f"w2l_{r}", [P, 3 * D], F32R) for r in range(2)]

        ident = sb("ident", [P, P])
        before = sb("before", [P, P], BF16)
        ones = sb("ones", [P, P], BF16)
        zeros = sb("zeros", [P, D])
        maskb = sb("maskb", [P, B * M], U8)
        maskf = sb("maskf", [P, B, M])
        maskn = sb("maskn", [P, M])
        valid = sb("valid", [P, B])
        mhalf = sb("mhalf", [P, 1])
        eio_i = sb("eio_i", [P, E], I32)
        eio = sb("eio", [P, E])
        ids = sb("ids", [P, B], I32)
        dflt = sb("dflt", [P, E, 2], I32)
        graw = sb("graw", [P, KD * E])
        gh = sb("gh", [P, KD * E], F32R)
        gl = sb("gl", [P, KD * E], F32R)

        x_in = [sb(f"x_in{p}", [P, D]) for p in range(2)]
        c_in = [sb(f"c_in{p}", [P, D]) for p in range(2)]
        ct_in = [sb(f"ct_in{p}", [P, D]) for p in range(2)]
        xn = sb("xn", [P, D])
        xnT = sb("xnT", [P, D])
        st1 = sb("st1", [P, 6])
        ag1 = sb("ag1", [P, 2])
        ve1 = sb("ve1", [P, 1])
        rs1 = sb("rs1", [P, 1])
        sm = sb("sm", [P, M])
        sn = sb("sn", [P, M])
        smin = sb("smin", [P, 1])
        pr = sb("pr", [P, M])
        rsum = sb("rsum", [P, 1])
        rinv = sb("rinv", [P, 1])
        rval = sb("rval", [P, 1])
        pT = sb("pT", [P, P])
        x2 = [sb(f"x2_{p}", [P, D]) for p in range(2)]
        x2n = [sb(f"x2n_{p}", [P, D]) for p in range(2)]
        st2 = sb("st2", [P, 6])
        ag2 = sb("ag2", [P, 2])
        ve2 = sb("ve2", [P, 1])
        rs2 = sb("rs2", [P, 1])

        top8 = sb("top8", [P, 8])
        idx8 = sb("idx8", [P, 8], U32)
        ntop = sb("ntop", [P, 1])
        etop = sb("etop", [P, 8])
        elog = sb("elog", [P, E])
        esum = sb("esum", [P, 1])
        einv = sb("einv", [P, 1])
        oh = sb("oh", [P, K, E], BF16)
        posx = sb("posx", [P, E])
        taken = sb("taken", [P, E])
        ohp = sb("ohp", [P, K, E])
        slot = [sb(f"slot{p}", [P, K], I32) for p in range(2)]
        vals = [sb(f"vals{p}", [P, K, 2], I32) for p in range(2)]

        tTh = sb("tTh", [P, D], F32R)
        tTl = sb("tTl", [P, D], F32R)
        act = sb("act", [P, I])
        gated = sb("gated", [P, I])
        h = sb("h", [P, I])
        hTh = sb("hTh", [P, 3 * P], F32R)
        hTl = sb("hTl", [P, 3 * P], F32R)
        xe = [*x_in, *c_in]
        y = [sb(f"y{p}", [P, D]) for p in range(2)]
        tabs = sb("tabs", [P, E, 2], I32)
        from4 = sb("from4", [P, 4], I32)
        to4 = sb("to4", [P, 4], I32)
        gate4 = sb("gate4", [P, 4])

        UP = [[bank(f"up1_{p}"), bank(f"up3_{p}")] for p in range(2)]
        HT = bank("hT_ps")
        YB = bank("y_ps")
        TB = bank("tT_ps")
        AT = bank("attention_ps")
        LG, BE, ALL = TB[:, 0:E], TB[:, E:2 * E], TB[:, 2 * E:3 * E]

        const_step = sem("const_step")
        const_ready = sem("const_ready")
        mask_in = sem("mask_in")
        gate_in = sem("gate_in")
        mask_ready = sem("mask_ready")
        gateh_ready = sem("gateh_ready")
        gatel_ready = sem("gatel_ready")
        x_ld = [sem(f"x_ld{p}") for p in range(2)]
        c_ld = [sem(f"c_ld{p}") for p in range(2)]
        raw13_in = [sem(f"raw13_in{r}") for r in range(RAW)]
        raw2_in = [sem(f"raw2_in{r}") for r in range(RAW)]
        wh13 = sem("wh13")
        wl13 = sem("wl13")
        wh2 = sem("wh2")
        wl2 = sem("wl2")
        ln1_link = sem("ln1_link")
        var1_ready = sem("var1_ready")
        rstd1_ready = sem("rstd1_ready")
        xn_ready = sem("xn_ready")
        xnT_done = sem("xnT_done")
        xnT_ready = sem("xnT_ready")
        scores_done = sem("scores_done")
        soft_link = sem("soft_link")
        soft_ready = sem("soft_ready")
        probs_ready = sem("probs_ready")
        pT_done = sem("pT_done")
        pT_ready = sem("pT_ready")
        read_done = sem("read_done")
        x2_ready = sem("x2_ready")
        ln2_link = sem("ln2_link")
        var2_ready = sem("var2_ready")
        rstd2_ready = sem("rstd2_ready")
        x2n_ready = sem("x2n_ready")
        tT_done = sem("tT_done")
        tTh_ready = sem("tTh_ready")
        tTl_ready = sem("tTl_ready")
        logits_done = sem("logits_done")
        top_link = sem("top_link")
        top_ready = sem("top_ready")
        etop_ready = sem("etop_ready")
        oh_ready = sem("oh_ready")
        pos_done = sem("pos_done")
        pos_read = sem("pos_read")
        slot_link = sem("slot_link")
        vals_ready = sem("vals_ready")
        table_init = sem("table_init")
        rows_init = sem("rows_init")
        table_st = [sem(f"table_st{p}") for p in range(2)]
        up_done = sem("up_done")
        tanh_ready = sem("tanh_ready")
        gated_link = sem("gated_link")
        h_ready = sem("h_ready")
        hT_done = sem("hT_done")
        hTh_ready = sem("hTh_ready")
        hTl_ready = sem("hTl_ready")
        down_done = sem("down_done")
        sum_ready = sem("sum_ready")
        tok_st = [sem(f"tok_st{p}") for p in range(2)]
        sum_st = [sem(f"sum_st{p}") for p in range(2)]
        table_in = sem("table_in")
        from_link = sem("from_link")
        gate_link = sem("gate_link")
        gates_ready = sem("gates_ready")
        xe_in = [sem(f"xe_in{q}") for q in range(4)]
        bxT_done = sem("bxT_done")
        bxTh_ready = sem("bxTh_ready")
        bxTl_ready = sem("bxTl_ready")
        bup_done = sem("bup_done")
        bsilu_ready = sem("bsilu_ready")
        bh_ready = sem("bh_ready")
        bhT_done = sem("bhT_done")
        bhTh_ready = sem("bhTh_ready")
        bhTl_ready = sem("bhTl_ready")
        bdown_done = sem("bdown_done")
        by_ready = sem("by_ready")
        added = sem("added")
        out_st = sem("out_st")

        block = es.enter_context(nc.Block())

        def even_odd(eng, first, pairs, step):
            with eng.Fori(0, pairs) as g:
                for j in range(2):
                    step(g * 2 + (first + j), (first + j) % 2, g + (first + j) // 2)

        def by_four(eng, first, fours, step):
            with eng.Fori(first // 4, first // 4 + fours) as g:
                for j in range(4):
                    step(g * 4 + j, j, g)

        def settled(eng):
            eng.nop(nofuse=True)

        @block.sync
        def _(sp):
            def load_chunk(c, p):
                sp.dma_start(x_in[p][:, :], x[c]).then_inc(x_ld[p], 16)
                sp.dma_start(ct_in[p][:, :].rearrange("p (k m) -> p k m", k=KD), ctx_t[c]).then_inc(c_ld[p], 16)
                sp.dma_start(c_in[p][:, :], ctx[c]).then_inc(c_ld[p], 16)

            def load_unit13(w, r):
                sp.dma_start(raw13[r][:, :].rearrange("p (k i) -> p k i", k=KD), w13[w]).then_inc(raw13_in[r], 16)

            def load_unit2(w, r):
                sp.dma_start(raw2[r][:, 0:2 * D].rearrange("p (c n) -> p c n", c=2), w2ab[w]).then_inc(raw2_in[r], 16)
                sp.dma_start(raw2[r][0:IC[2][1], 2 * D:3 * D], w2c[w]).then_inc(raw2_in[r], 16)

            def reload_unit(w, r, use):
                r1, use1 = (r - 1) % RAW, use - (r == 0)
                sp.wait_ge(wl13, w * 2 - 6)
                sp.wait_ge(raw13_in[r1], use1 * 16 + 16)
                load_unit13(w, r)
                sp.wait_ge(wl2, w * 2 - 6)
                sp.wait_ge(raw2_in[r1], use1 * 32 + 32)
                load_unit2(w, r)

            def step(c, p, half, load=True, attend=True, shared=True):
                if attend:
                    sp.wait_ge(x2n_ready, c + 1)
                    sp.dma_start(tokens[bass.ds(c * P, P), :], x2n[p][:, :]).then_inc(tok_st[p], 16)
                if load:
                    load_chunk(c + 2, p)
                if shared:
                    sp.wait_ge(sum_ready, c)
                    sp.dma_start(total[bass.ds((c - 1) * P, P), :], y[1 - p][:, :]).then_inc(sum_st[1 - p], 16)

            load_chunk(0, 0)
            sp.dma_start(maskb[:, :], mask.rearrange("b m -> (b m)").partition_broadcast(P)).then_inc(mask_in, 16)
            sp.dma_start(graw[:, :].rearrange("p (k e) -> p k e", k=KD), gate_t).then_inc(gate_in, 16)
            load_chunk(1, 1)
            for w in range(RAW):
                load_unit13(w, w)
                load_unit2(w, w)
            step(0, 0, 0, shared=False)
            step(1, 1, 0)
            reload_unit(4, 0, 1)
            reload_unit(5, 1, 1)
            even_odd(sp, 2, (B - 4) // 2, step)
            step(B - 2, 0, B // 2 - 1, load=False)
            step(B - 1, 1, B // 2 - 1, load=False)
            step(B, 0, B // 2, load=False, attend=False)
            with sp.Fori(0, (UNITS - 6) // 4) as g:
                for j in range(4):
                    reload_unit(g * 4 + (6 + j), (6 + j) % 4, g + (6 + j) // 4)
            assert (UNITS - 6) % 4 == 0
            sp.wait_ge(added, 16 * E)
            sp.dma_start(out.rearrange("b s d -> (b s) d"), total[0:N, :]).then_inc(out_st, 16)
            sp.wait_ge(out_st, 16)

        @block.gpsimd
        def _(pool):
            n = [0]

            def made(ins):
                n[0] += 1
                ins.then_inc(const_step, 1)

            made(pool.memset(ident[:, :], 0.0))
            made(pool.memset(before[:, :], 1.0))
            made(pool.memset(ones[:, :], 1.0))
            made(pool.memset(zeros[:, :], 0.0))
            made(pool.memset(mhalf[:, :], -0.5))
            made(pool.memset(dflt[:, :, :], 0))
            made(pool.iota(eio_i[:, :], pattern=[[1, E]], base=0, channel_multiplier=0))
            made(pool.iota(ids[:, :], pattern=[[P, B]], base=0, channel_multiplier=1))
            pool.wait_ge(const_step, n[0])
            made(pool.affine_select(out=ident[:, :], in_=ident[:, :], compare_op=ALU.not_equal, fill=1.0,
                                    base=0, pattern=[[-1, P]], channel_multiplier=1))
            made(pool.affine_select(out=before[:, :], in_=before[:, :], compare_op=ALU.is_gt, fill=0.0,
                                    base=0, pattern=[[1, P]], channel_multiplier=-1))
            made(pool.iota(dflt[:, :, 0], pattern=[[0, E]], base=N, channel_multiplier=1))
            pool.wait_ge(const_step, n[0])
            pool.sem_inc(const_ready, 1)
            pool.dma_start(table.rearrange("(p e) two -> p (e two)", p=P),
                           dflt[:, :, :].rearrange("p e two -> p (e two)")).then_inc(table_init, 16)
            pool.dma_start(tokens[N:N + CAP, :], zeros[:, :]).then_inc(rows_init, 16)
            pool.dma_start(total[N:N + CAP, :], zeros[:, :]).then_inc(rows_init, 16)

            def rstd(c, var_ready, ve, rs, ready):
                pool.wait_ge(var_ready, c + 1)
                pool.tensor_tensor(rs[:, :], ve[:, :], mhalf[:, :], ALU.pow).then_inc(ready, 1)

            def slots(p, first, last):
                for k in range(first, last):
                    pool.indirect_dma_start(
                        out=table[:, :], out_offset=bass.IndirectOffsetOnAxis(ap=slot[p][:, k:k + 1], axis=0),
                        in_=vals[p][:, k, :], in_offset=None,
                        bounds_check=CAP * E - 1, oob_is_err=False).then_inc(table_st[p], 16)

            def step(c, p, half, attend=True, shared=True, ahead=True):
                if ahead:
                    rstd(c + 1, var1_ready, ve1, rs1, rstd1_ready)
                if shared:
                    pool.wait_ge(vals_ready, c)
                    settled(pool)
                    slots(1 - p, 0, 4)
                if attend:
                    rstd(c, var2_ready, ve2, rs2, rstd2_ready)
                if shared:
                    slots(1 - p, 4, K)

            rstd(0, var1_ready, ve1, rs1, rstd1_ready)
            pool.wait_ge(table_init, 16)
            step(0, 0, 0, shared=False)
            even_odd(pool, 1, (B - 2) // 2, step)
            step(B - 1, 1, B // 2 - 1, ahead=False)
            step(B, 0, B // 2, attend=False, ahead=False)

            for p in range(2):
                pool.wait_ge(table_st[p], 16 * K * B // 2)
            pool.dma_start(tabs[:, :, :].rearrange("p e two -> p (e two)"),
                           table.rearrange("(p e) two -> p (e two)", p=P)).then_inc(table_in, 16)
            pool.wait_ge(rows_init, 32)
            for p in range(2):
                pool.wait_ge(tok_st[p], 16 * B // 2)
                pool.wait_ge(sum_st[p], 16 * B // 2)

            def gather(e, q):
                pool.tensor_copy(from4[:, q:q + 1], tabs[:, bass.ds(e, 1), 0]).then_inc(from_link, 1)
                pool.wait_ge(from_link, e + 1)
                settled(pool)
                pool.indirect_dma_start(
                    out=xe[q][:, :], out_offset=None, in_=tokens[:, :],
                    in_offset=bass.IndirectOffsetOnAxis(ap=from4[:, q:q + 1], axis=0),
                    bounds_check=N + CAP - 1, oob_is_err=True).then_inc(xe_in[q], 16)

            def slots_of(e, q):
                pool.tensor_copy(to4[:, q:q + 1], tabs[:, bass.ds(e, 1), 0]).then_inc(gate_link, 1)
                pool.tensor_copy(gate4[:, q:q + 1], tabs[:, bass.ds(e, 1), 1].bitcast(F32)).then_inc(gates_ready, 1)

            def scatter(e, q):
                pool.wait_ge(gate_link, e + 1)
                pool.wait_ge(by_ready, e + 1)
                settled(pool)
                pool.indirect_dma_start(
                    out=total[:, :], out_offset=bass.IndirectOffsetOnAxis(ap=to4[:, q:q + 1], axis=0),
                    in_=y[q % 2][:, :], in_offset=None,
                    bounds_check=N + CAP - 1, oob_is_err=True, compute_op=ALU.add).then_inc(added, 16)

            pool.wait_ge(table_in, 16)
            for e in range(4):
                gather(e, e)
            slots_of(0, 0)
            slots_of(1, 1)

            def expert(e, q, g=None, ahead=True, behind=True, first=False):
                if ahead:
                    pool.wait_ge(bxT_done, e + 1)
                    settled(pool)
                    gather(e + 4, q)
                if behind:
                    if not first:
                        pool.wait_ge(added, (e - 1) * 16)
                    scatter(e - 1, (q - 1) % 4)
                if not (isinstance(e, int) and e + 2 >= E):
                    slots_of(e + 2, (q + 2) % 4)

            expert(0, 0, behind=False)
            expert(1, 1, first=True)
            expert(2, 2)
            expert(3, 3)
            by_four(pool, 4, E // 4 - 2, expert)
            for e in range(E - 4, E):
                expert(e, e % 4, ahead=False)
            pool.wait_ge(added, 16 * (E - 1))
            scatter(E - 1, (E - 1) % 4)
            pool.wait_ge(added, 16 * E)

        @block.scalar
        def _(ac):
            def split13(r, q, use, free, halves=(0, 1)):
                if 0 in halves:
                    ac.wait_ge(raw13_in[r], use * 16 + 16)
                    free()
                n = KD * I
                for a in halves:
                    ac.activation(w13h[q][:, a * n:(a + 1) * n], raw13[r][:, a * n:(a + 1) * n],
                                  ACT.Copy).then_inc(wh13, 1)

            def split2(r, q, use, free):
                ac.wait_ge(raw2_in[r], use * 32 + 32)
                free()
                ac.activation(w2h[q][:, 0:2 * D], raw2[r][:, 0:2 * D], ACT.Copy).then_inc(wh2, 1)
                ac.activation(w2h[q][0:IC[2][1], 2 * D:3 * D], raw2[r][0:IC[2][1], 2 * D:3 * D],
                              ACT.Copy).then_inc(wh2, 1)

            def hi_of_hT(done, at, freed, free_at, ready):
                ac.wait_ge(done, at)
                if free_at is not None:
                    ac.wait_ge(freed, free_at)
                ac.activation(hTh[:, 0:2 * P], HT[:, 0:2 * P], ACT.Copy)
                ac.activation(hTh[0:IC[2][1], 2 * P:3 * P], HT[0:IC[2][1], 2 * P:3 * P], ACT.Copy).then_inc(ready, 1)

            def shared_half(s, u, first):
                ac.wait_ge(up_done, s * 2 + (u + 1))
                if not (first and u == 0):
                    ac.wait_ge(h_ready, s * 2 + u)
                ac.activation(act[:, :], UP[u][0][:, 0:I], ACT.Tanh, scale=0.5).then_inc(tanh_ready, 1)

            def shared_hT(s, u, first):
                hi_of_hT(hT_done, s * 2 + (u + 1), down_done, None if first and u == 0 else s * 2 + u, hTh_ready)

            def copy_xnT(c, first=False):
                ac.wait_ge(xnT_done, c + 1)
                if not first:
                    ac.wait_ge(scores_done, c)
                ac.activation(xnT[:, :], AT[:, :], ACT.Copy).then_inc(xnT_ready, 1)

            def step(c, p, half, attend=True, shared=True, first=False, ahead=True):
                s = c - 1
                if attend:
                    ac.wait_ge(soft_ready, c + 1)
                    if shared:
                        ac.wait_ge(pT_done, c)
                    ac.activation(pr[:, :], sn[:, :], ACT.Exp, bias=smin[:, :], scale=-1.0,
                                  accum_out=rsum[:, :]).then_inc(probs_ready, 1)
                if shared:
                    ac.wait_ge(top_ready, s + 1)
                    ac.activation(elog[:, :], LG, ACT.Exp, bias=ntop[:, :], accum_out=esum[:, :])
                    ac.activation(etop[:, :], top8[:, :], ACT.Exp, bias=ntop[:, :]).then_inc(etop_ready, 1)
                    shared_half(s, 0, first)
                    shared_hT(s, 0, first)
                    shared_half(s, 1, first)
                    shared_hT(s, 1, first)
                if ahead:
                    copy_xnT(c + 1)
                if attend:
                    ac.wait_ge(tT_done, c + 1)
                    if shared:
                        ac.wait_ge(up_done, c * 2)
                    ac.activation(tTh[:, :], TB[:, :], ACT.Copy).then_inc(tTh_ready, 1)

            copy_xnT(0, first=True)
            ac.wait_ge(gate_in, 16)
            ac.activation(gh[:, :], graw[:, :], ACT.Copy).then_inc(gateh_ready, 1)
            step(0, 0, 0, shared=False, first=True)
            for w in range(SHARED):
                split13(w, w, 0, lambda: None)
                split2(w, w, 0, lambda: None)
            step(1, 1, 0, first=True)
            step(2, 0, 1)
            even_odd(ac, 3, (B - 4) // 2, step)
            step(B - 1, 1, B // 2 - 1, ahead=False)
            step(B, 0, B // 2, attend=False, ahead=False)

            def silu(e, q, first=False):
                ac.wait_ge(bup_done, e + 1)
                if not first:
                    ac.wait_ge(bh_ready, e)
                ac.activation(act[:, :], UP[q % 2][0][:, 0:I], ACT.Silu).then_inc(bsilu_ready, 1)

            def hi_of_x(e, free):
                ac.wait_ge(bxT_done, e + 1)
                free()
                ac.activation(tTh[:, :], TB[:, :], ACT.Copy).then_inc(bxTh_ready, 1)

            def weigh(e, q, wait_added=True):
                ac.wait_ge(bdown_done, e + 1)
                ac.wait_ge(gates_ready, e + 1)
                if wait_added:
                    ac.wait_ge(added, (e - 1) * 16)
                ac.activation(y[q % 2][:, :], YB[:, :], ACT.Copy, scale=gate4[:, q:q + 1]).then_inc(by_ready, 1)

            def down_free(e):
                if isinstance(e, int) and e < 2:
                    ac.wait_ge(down_done, 2 * B - 1 + e)
                else:
                    ac.wait_ge(bdown_done, e - 1)

            def up_free(e):
                if isinstance(e, int) and e < 2:
                    ac.wait_ge(up_done, 2 * B - 1 + e)
                else:
                    ac.wait_ge(bup_done, e - 1)

            def expert(e, q, g, ahead=True, behind=True):
                if behind:
                    hi_of_hT(bhT_done, e, bdown_done, None if isinstance(e, int) and e == 1 else e - 1, bhTh_ready)
                    split2((q + 1) % 4, (q + 1) % 2, g + (q + 1) // 4, lambda: down_free(e - 1))
                if ahead:
                    split13((q + 3) % 4, (q + 1) % 2, g + (q + 3) // 4, lambda: up_free(e + 1), halves=(0,))
                silu(e, q, first=isinstance(e, int) and e == 0)
                if ahead:
                    hi_of_x(e + 1, lambda: ac.wait_ge(bup_done, e + 1))
                    split13((q + 3) % 4, (q + 1) % 2, None, None, halves=(1,))
                if behind:
                    weigh(e - 1, (q - 1) % 4, wait_added=not (isinstance(e, int) and e < 3))

            split13(2, 0, 0, lambda: up_free(0))
            hi_of_x(0, lambda: ac.wait_ge(up_done, 2 * B))
            for e in range(4):
                expert(e, e, 0, behind=e > 0)
            by_four(ac, 4, E // 4 - 2, expert)
            for e in range(E - 4, E):
                expert(e, e % 4, e // 4, ahead=e + 1 < E)
            hi_of_hT(bhT_done, E, bdown_done, E - 1, bhTh_ready)
            split2((E + 1) % 4, (E + 1) % 2, (E + 1) // 4, lambda: down_free(E - 1))
            weigh(E - 1, (E - 1) % 4)

        @block.vector
        def _(ve):
            class Links:

                def __init__(self, s, n, step):
                    self.s, self.n, self.base, self.k = s, n, step * n, 0

                def done(self, ins):
                    ins.then_inc(self.s, 1)
                    self.k += 1
                    assert self.k <= self.n

                def wait(self):
                    ve.wait_ge(self.s, self.base + self.k)

            def split13(r, q, at, halves=(0, 1)):
                n = KD * I
                for a in halves:
                    ve.wait_ge(wh13, at + (a + 1))
                    ve.tensor_tensor(w13l[q][:, a * n:(a + 1) * n], raw13[r][:, a * n:(a + 1) * n],
                                     w13h[q][:, a * n:(a + 1) * n].bitcast(F32), ALU.subtract).then_inc(wl13, 1)

            def split2(r, q, at):
                parts = [(P, 0, 2 * D), (IC[2][1], 2 * D, 3 * D)]
                for a, (rows, lo, hi) in enumerate(parts):
                    ve.wait_ge(wh2, at + (a + 1))
                    ve.tensor_tensor(w2l[q][0:rows, lo:hi], raw2[r][0:rows, lo:hi],
                                     w2h[q][0:rows, lo:hi].bitcast(F32), ALU.subtract).then_inc(wl2, 1)

            def lo_of_hT(hi_ready, at, ready):
                ve.wait_ge(hi_ready, at)
                ve.tensor_tensor(hTl[:, 0:2 * P], HT[:, 0:2 * P], hTh[:, 0:2 * P].bitcast(F32), ALU.subtract)
                n = IC[2][1]
                ve.tensor_tensor(hTl[0:n, 2 * P:3 * P], HT[0:n, 2 * P:3 * P], hTh[0:n, 2 * P:3 * P].bitcast(F32),
                                 ALU.subtract).then_inc(ready, 1)

            def lo_of_x(hi_ready, at, ready):
                ve.wait_ge(hi_ready, at)
                ve.tensor_tensor(tTl[:, :], TB[:, :], tTh[:, :].bitcast(F32), ALU.subtract).then_inc(ready, 1)

            def norm_stats(c, src, st, ag, vv, link, ready):
                ln = Links(link, 2, c)
                ln.done(ve.bn_stats(st[:, :], src))
                ln.wait()
                settled(ve)
                ln.done(ve.bn_aggr(ag[:, :], st[:, :]))
                ln.wait()
                ve.tensor_scalar(vv[:, :], ag[:, 1:2], EPS, None, ALU.add).then_inc(ready, 1)

            def norm1_stats(c, p, half):
                ve.wait_ge(x_ld[p], half * 16 + 16)
                norm_stats(c, x_in[p][:, :], st1, ag1, ve1, ln1_link, var1_ready)

            def norm1_apply(c, p, first=False):
                ve.wait_ge(rstd1_ready, c + 1)
                if not first:
                    ve.wait_ge(xnT_done, c)
                ve.tensor_scalar(xn[:, :], x_in[p][:, :], ag1[:, 0:1], rs1[:, 0:1], ALU.subtract,
                                 ALU.mult).then_inc(xn_ready, 1)

            def route_top(s):
                ve.wait_ge(logits_done, s + 1)
                settled(ve)
                ln = Links(top_link, 2, s)
                ln.done(ve.max(top8[:, :], LG))
                ln.wait()
                settled(ve)
                ln.done(ve.max_index(idx8[:, :], top8[:, :], LG))
                ve.tensor_scalar(ntop[:, :], top8[:, 0:1], -1.0, None, ALU.mult).then_inc(top_ready, 1)
                ln.wait()
                ve.tensor_tensor(oh[:, :, :], idx8[:, 0:K].unsqueeze(2).to_broadcast([P, K, E]),
                                 eio[:, :].unsqueeze(1).to_broadcast([P, K, E]), ALU.is_equal).then_inc(oh_ready, 1)

            def route_slots(s, p, half):
                ve.wait_ge(pos_done, s + 1)
                if not (isinstance(s, int) and s == 0):
                    ve.wait_ge(pos_read, s * 2)
                ve.scalar_tensor_tensor(posx[:, :], BE, float(E), taken[:, :], ALU.mult,
                                        ALU.add).then_inc(pos_read, 1)
                ve.wait_ge(pos_read, s * 2 + 1)
                ve.scalar_tensor_tensor(taken[:, :], ALL, float(E), taken[:, :], ALU.mult,
                                        ALU.add).then_inc(pos_read, 1)
                ve.wait_ge(etop_ready, s + 1)
                ve.reciprocal(einv[:, :], esum[:, :]).then_inc(slot_link, 1)
                if not (isinstance(s, int) and s < 2):
                    ve.wait_ge(table_st[p], half * (16 * K))
                ve.tensor_tensor(ohp[:, :, :], oh[:, :, :], posx[:, :].unsqueeze(1).to_broadcast([P, K, E]),
                                 ALU.mult).then_inc(slot_link, 1)
                ve.tensor_copy(vals[p][:, :, 0], ids[:, bass.ds(s, 1)].to_broadcast([P, K]))
                ve.wait_ge(slot_link, s * 2 + 2)
                ve.tensor_scalar(vals[p][:, :, 1].bitcast(F32), etop[:, 0:K], einv[:, 0:1], None, ALU.mult)
                with nc.allow_low_precision(reason="whole numbers under 2 ** 24, one of each row's nonzero"):
                    ve.tensor_reduce(slot[p][:, :], ohp[:, :, :], AX.X, ALU.add).then_inc(vals_ready, 1)

            def gate_begin(s, u):
                ve.wait_ge(tanh_ready, s * 2 + (u + 1))
                ve.scalar_tensor_tensor(gated[:, :], act[:, :], 1.0, UP[u][0][:, 0:I], ALU.add,
                                        ALU.mult).then_inc(gated_link, 1)

            def gate_end(s, u):
                if not (isinstance(s, int) and s == 0 and u == 0):
                    ve.wait_ge(hT_done, s * 2 + u)
                ve.wait_ge(gated_link, s * 2 + (u + 1))
                ve.scalar_tensor_tensor(h[:, :], gated[:, :], 0.5, UP[u][1][:, 0:I], ALU.mult,
                                        ALU.mult).then_inc(h_ready, 1)

            def store_sum(s, p, half):
                ve.wait_ge(down_done, s * 2 + 2)
                if not (isinstance(s, int) and s < 2):
                    ve.wait_ge(sum_st[p], half * 16)
                ve.tensor_tensor(y[p][:, :], YB[:, :], x2[p][:, :], ALU.add).then_inc(sum_ready, 1)

            def step(c, p, half, attend=True, shared=True, ahead=True):
                s, ps = c - 1, 1 - p
                halfs = half - 1 + p
                if attend:
                    ve.tensor_scalar(maskn[:, :], maskf[:, bass.ds(c, 1), :].squeeze(1), -BIG, BIG, ALU.mult, ALU.add)
                    ve.wait_ge(scores_done, c + 1)
                    ve.scalar_tensor_tensor(sm[:, :], AT[:, 0:M], -SCALE, maskf[:, bass.ds(c, 1), :].squeeze(1),
                                            ALU.mult, ALU.mult).then_inc(soft_link, 1)
                    ve.wait_ge(soft_link, c + 1)
                    settled(ve)
                    ve.tensor_tensor_reduce(out=sn[:, :], in0=sm[:, :], in1=maskn[:, :],
                                            scale=1.0, scalar=HUGE, op0=ALU.add, op1=ALU.min,
                                            accum_out=smin[:, :]).then_inc(soft_ready, 1)
                if not (isinstance(s, int) and s < 1):
                    store_sum(s - 1, p, half - 1)
                if shared:
                    route_top(s)
                if ahead:
                    norm1_stats(c + 1, 1 - p, half + p)
                if attend:
                    ve.wait_ge(probs_ready, c + 1)
                    ve.reciprocal(rinv[:, :], rsum[:, :]).then_inc(ln2_link, 1)
                if ahead:
                    norm1_apply(c + 1, 1 - p)
                if attend:
                    ve.wait_ge(ln2_link, c * 4 + 1)
                    ve.tensor_scalar(rval[:, :], rinv[:, :], valid[:, bass.ds(c, 1)], None,
                                     ALU.mult).then_inc(ln2_link, 1)
                if shared:
                    gate_begin(s, 0)
                if attend:
                    ve.wait_ge(pT_done, c + 1)
                    ve.tensor_copy(pT[:, :], AT[:, M:2 * M]).then_inc(pT_ready, 1)
                if shared:
                    gate_end(s, 0)
                    route_slots(s, ps, halfs)
                    lo_of_hT(hTh_ready, s * 2 + 1, hTl_ready)
                    gate_begin(s, 1)
                if attend:
                    ve.wait_ge(read_done, c + 1)
                    ve.wait_ge(ln2_link, c * 4 + 2)
                    ve.scalar_tensor_tensor(x2[p][:, :], AT[:, :], rval[:, :], x_in[p][:, :], ALU.mult,
                                            ALU.add).then_inc(x2_ready, 1)
                if shared:
                    gate_end(s, 1)
                if attend:
                    ve.wait_ge(x2_ready, c + 1)
                    ve.bn_stats(st2[:, :], x2[p][:, :]).then_inc(ln2_link, 1)
                    ve.wait_ge(ln2_link, c * 4 + 3)
                    settled(ve)
                    ve.bn_aggr(ag2[:, :], st2[:, :]).then_inc(ln2_link, 1)
                    ve.wait_ge(ln2_link, c * 4 + 4)
                    ve.tensor_scalar(ve2[:, :], ag2[:, 1:2], EPS, None, ALU.add).then_inc(var2_ready, 1)
                if shared:
                    lo_of_hT(hTh_ready, s * 2 + 2, hTl_ready)
                if attend:
                    ve.wait_ge(rstd2_ready, c + 1)
                    if not (isinstance(c, int) and c < 2):
                        ve.wait_ge(tok_st[p], half * 16)
                    ve.tensor_scalar(x2n[p][:, :], x2[p][:, :], ag2[:, 0:1], rs2[:, 0:1], ALU.subtract,
                                     ALU.mult).then_inc(x2n_ready, 1)
                    lo_of_x(tTh_ready, c + 1, tTl_ready)

            norm1_stats(0, 0, 0)
            norm1_apply(0, 0, first=True)
            ve.wait_ge(mask_in, 16)
            ve.tensor_copy(maskf[:, :, :].rearrange("p b m -> p (b m)"), maskb[:, :]).then_inc(mask_ready, 1)
            ve.wait_ge(mask_ready, 1)
            ve.tensor_reduce(valid[:, :], maskf[:, :, :], AX.X, ALU.max).then_inc(mask_ready, 1)
            ve.wait_ge(const_ready, 1)
            ve.tensor_copy(eio[:, :], eio_i[:, :]).then_inc(mask_ready, 1)
            ve.tensor_copy(taken[:, :], eio_i[:, :]).then_inc(mask_ready, 1)
            ve.wait_ge(mask_ready, 4)
            ve.wait_ge(gateh_ready, 1)
            ve.tensor_tensor(gl[:, :], graw[:, :], gh[:, :].bitcast(F32), ALU.subtract).then_inc(gatel_ready, 1)
            step(0, 0, 0, shared=False)
            for w in range(SHARED):
                split13(w, w, 2 * w)
                split2(w, w, 2 * w)
            step(1, 1, 0)
            step(2, 0, 1)
            even_odd(ve, 3, (B - 4) // 2, step)
            step(B - 1, 1, B // 2 - 1, ahead=False)
            step(B, 0, B // 2, attend=False, ahead=False)
            store_sum(B - 1, 1, B // 2 - 1)

            def gate(e, q, first=False):
                ve.wait_ge(bsilu_ready, e + 1)
                if not first:
                    ve.wait_ge(bhT_done, e)
                ve.tensor_tensor(h[:, :], act[:, :], UP[q % 2][1][:, 0:I], ALU.mult).then_inc(bh_ready, 1)

            def expert(e, q, g=None, ahead=True, behind=True):
                if behind:
                    lo_of_hT(bhTh_ready, e, bhTl_ready)
                    split2((q + 1) % 4, (q + 1) % 2, (e + 1) * 2)
                if ahead:
                    split13((q + 3) % 4, (q + 1) % 2, (e + 3) * 2, halves=(0,))
                gate(e, q, first=isinstance(e, int) and e == 0)
                if ahead:
                    lo_of_x(bxTh_ready, e + 2, bxTl_ready)
                    split13((q + 3) % 4, (q + 1) % 2, (e + 3) * 2, halves=(1,))

            split13(2, 0, 4)
            lo_of_x(bxTh_ready, 1, bxTl_ready)
            for e in range(4):
                expert(e, e, behind=e > 0)
            by_four(ve, 4, E // 4 - 2, expert)
            for e in range(E - 4, E):
                expert(e, e % 4, ahead=e + 1 < E)
            lo_of_hT(bhTh_ready, E, bhTl_ready)
            split2((E + 1) % 4, (E + 1) % 2, (E + 1) * 2)

        @block.tensor
        def _(pe):
            def transpose4(dst, src):
                for k in range(KD):
                    last = pe.transpose(dst[:, k * P:(k + 1) * P], src[:, k * P:(k + 1) * P], ident[:, :])
                return last

            def transpose_h():
                for j, (lo, n) in enumerate(IC):
                    last = pe.transpose(HT[0:n, j * P:(j + 1) * P], h[:, lo:lo + n], ident[:, :])
                return last

            def up(q, banks, halves=(0, 1), halfway=lambda: None):
                for k in range(KD):
                    if k // (KD // 2) not in halves:
                        continue
                    if k == KD // 2:
                        halfway()
                    for a, b in ((tTh, w13h[q]), (tTh, w13l[q]), (tTl, w13h[q])):
                        for v in range(2):
                            o = (2 * k + v) * I
                            last = pe.matmul(banks[v][:, 0:I], a[:, k * P:(k + 1) * P], b[:, o:o + I],
                                             start=(k == 0 and a is tTh and b is w13h[q]),
                                             stop=(k == KD - 1 and a is tTl))
                return last

            def down(q, start=True, stop=True):
                for j, (lo, n) in enumerate(IC):
                    for a, b in ((hTh, w2h[q]), (hTh, w2l[q]), (hTl, w2h[q])):
                        last = pe.matmul(YB[:, :], a[0:n, j * P:(j + 1) * P], b[0:n, j * D:(j + 1) * D],
                                         start=(start and j == 0 and a is hTh and b is w2h[q]),
                                         stop=(stop and j == 2 and a is hTl))
                return last

            def count(dst, sel):
                for k in range(K):
                    last = pe.matmul(dst, sel[:, :], oh[:, k, :], start=(k == 0), stop=(k == K - 1))
                return last

            def shared_hT(s, u):
                pe.wait_ge(h_ready, s * 2 + (u + 1))
                if not (isinstance(s, int) and s == 0 and u == 0):
                    pe.wait_ge(hTl_ready, s * 2 + u)
                transpose_h().then_inc(hT_done, 1)

            def shared_down(s, u, weights=False):
                pe.wait_ge(hTl_ready, s * 2 + (u + 1))
                if u == 0 and not (isinstance(s, int) and s == 0):
                    pe.wait_ge(sum_ready, s)
                if weights:
                    pe.wait_ge(wl2, 2 * u + 2)
                down(u, start=(u == 0), stop=(u == 1)).then_inc(down_done, 1)

            def transpose_xn(c):
                pe.wait_ge(xn_ready, c + 1)
                if not (isinstance(c, int) and c == 0):
                    pe.wait_ge(x2_ready, c)
                transpose4(AT, xn).then_inc(xnT_done, 1)

            def step(c, p, half, attend=True, shared=True, ahead=True, weights=False):
                s = c - 1
                after_first = not (isinstance(s, int) and s == 0)
                if attend:
                    pe.wait_ge(xnT_ready, c + 1)
                    pe.wait_ge(c_ld[p], half * 32 + 32)
                    for k in range(KD):
                        last = pe.matmul(AT[:, 0:M], xnT[:, k * P:(k + 1) * P], ct_in[p][:, k * M:(k + 1) * M],
                                         start=(k == 0), stop=(k == KD - 1))
                    last.then_inc(scores_done, 1)
                if shared:
                    pe.wait_ge(tTl_ready, s + 1)
                    for k in range(KD):
                        for a, b in ((tTh, gh), (tTh, gl), (tTl, gh)):
                            last = pe.matmul(LG, a[:, k * P:(k + 1) * P], b[:, k * E:(k + 1) * E],
                                             start=(k == 0 and a is tTh and b is gh), stop=(k == KD - 1 and a is tTl))
                    last.then_inc(logits_done, 1)
                    if weights:
                        pe.wait_ge(wl13, 1)
                    if after_first:
                        pe.wait_ge(h_ready, s * 2 - 1)
                    up(0, UP[0], halfway=(lambda: pe.wait_ge(wl13, 2)) if weights else (lambda: None))\
                        .then_inc(up_done, 1)
                if attend:
                    pe.wait_ge(probs_ready, c + 1)
                    pe.transpose(AT[:, M:2 * M], pr[:, :], ident[:, :]).then_inc(pT_done, 1)
                if shared:
                    pe.wait_ge(oh_ready, s + 1)
                    pe.wait_ge(etop_ready, s + 1)
                    count(BE, before)
                    count(ALL, ones).then_inc(pos_done, 1)
                    if weights:
                        pe.wait_ge(wl13, 4)
                    if after_first:
                        pe.wait_ge(h_ready, s * 2)
                    up(1, UP[1], halves=(0,))
                    shared_hT(s, 0)
                    up(1, UP[1], halves=(1,)).then_inc(up_done, 1)
                if attend:
                    pe.wait_ge(pT_ready, c + 1)
                    pe.matmul(AT[:, :], pT[:, :], c_in[p][:, :], start=True, stop=True).then_inc(read_done, 1)
                if shared:
                    shared_down(s, 0, weights)
                    shared_hT(s, 1)
                if ahead:
                    transpose_xn(c + 1)
                if attend:
                    pe.wait_ge(x2n_ready, c + 1)
                    if shared:
                        pe.wait_ge(pos_read, s * 2 + 2)
                    transpose4(TB, x2n[p]).then_inc(tT_done, 1)
                if shared:
                    shared_down(s, 1, weights)

            pe.wait_ge(const_ready, 1)
            transpose_xn(0)
            step(0, 0, 0, shared=False)
            pe.wait_ge(gatel_ready, 1)
            step(1, 1, 0, weights=True)
            even_odd(pe, 2, (B - 4) // 2, step)
            step(B - 2, 0, B // 2 - 1)
            step(B - 1, 1, B // 2 - 1, ahead=False)
            step(B, 0, B // 2, attend=False, ahead=False)

            def transpose_x(loaded, q):
                pe.wait_ge(xe_in[q], loaded)
                transpose4(TB, xe[q]).then_inc(bxT_done, 1)

            def expert(e, q, g, ahead=True, behind=True):
                pe.wait_ge(bxTl_ready, e + 1)
                if not (isinstance(e, int) and e < 2):
                    pe.wait_ge(bh_ready, e - 1)
                pe.wait_ge(wl13, (e + 2) * 2 + 1)
                up(q % 2, UP[q % 2], halfway=lambda: pe.wait_ge(wl13, (e + 2) * 2 + 2)).then_inc(bup_done, 1)
                if ahead:
                    transpose_x((g + (q + 1) // 4) * 16 + 16, (q + 1) % 4)
                if behind:
                    pe.wait_ge(bhTl_ready, e)
                    pe.wait_ge(wl2, (e + 2) * 2)
                    if not (isinstance(e, int) and e < 2):
                        pe.wait_ge(by_ready, e - 1)
                    down((q - 1) % 2).then_inc(bdown_done, 1)
                pe.wait_ge(bh_ready, e + 1)
                transpose_h().then_inc(bhT_done, 1)

            transpose_x(16, 0)
            for e in range(4):
                expert(e, e, 0, behind=e > 0)
            by_four(pe, 4, E // 4 - 2, expert)
            for e in range(E - 4, E):
                expert(e, e % 4, e // 4, ahead=e + 1 < E)
            pe.wait_ge(bhTl_ready, E)
            pe.wait_ge(wl2, (E + 2) * 2)
            pe.wait_ge(by_ready, E - 1)
            down((E - 1) % 2).then_inc(bdown_done, 1)


def kernel(**inputs):
    import numpy as _np
    import concourse.bacc as _bacc
    from concourse import mybir as _mybir
    from concourse.bass_utils import run_bass_kernel_spmd as _run

    x = _np.ascontiguousarray(inputs["x"])
    ctx = _np.ascontiguousarray(inputs["ctx_2048"])
    mask = _np.ascontiguousarray(inputs["mask_BxS2_bk0"])
    gate_w, w1, w2, w3, sw1, sw2, sw3 = (
        _np.asarray(inputs["L0_ffn_" + n]) for n in ("gate_w", "w1", "w2", "w3", "sw1", "sw2", "sw3"))
    B, S, D = x.shape
    E, I, _ = w1.shape
    kd, n2 = D // 128, sw1.shape[0] // I
    a1 = _np.concatenate([sw1.reshape(n2, I, D), w1])
    a3 = _np.concatenate([sw3.reshape(n2, I, D), w3])
    a2 = _np.concatenate([sw2.reshape(D, n2, I).transpose(1, 0, 2), w2])
    w13 = _np.stack([a1, a3], axis=1).reshape(n2 + E, 2 * I, kd, 128).transpose(0, 3, 2, 1)
    a2 = a2.transpose(0, 2, 1)
    arrays = {
        "x": x,
        "ctx": ctx,
        "ctx_t": ctx.reshape(B, S, kd, 128).transpose(0, 3, 2, 1),
        "mask": mask,
        "gate_t": gate_w.reshape(E, kd, 128).transpose(2, 1, 0),
        "w13": w13,
        "w2ab": a2[:, 0:256].reshape(n2 + E, 2, 128, D).transpose(0, 2, 1, 3),
        "w2c": a2[:, 256:],
    }
    nc = _bacc.Bacc("TRN2", target_bir_lowering=False, num_devices=1)
    args, ins = [], {}
    for name, a in arrays.items():
        a = _np.ascontiguousarray(a)
        ins[f"in_{name}"] = a
        args.append(nc.dram_tensor(f"in_{name}", a.shape, _mybir.dt.from_np(a.dtype), kind="ExternalInput").ap())
    args.append(nc.dram_tensor("out_0", (B, S, D), _mybir.dt.float32, kind="ExternalOutput").ap())
    cross_attention_moe_kernel(nc, *args)
    r = _run(nc, [ins], core_ids=[0])
    return r.results[0]["out_0"]
```

```python
import concourse.bass as bass
from concourse import mybir
from contextlib import ExitStack


def cross_attention_moe_kernel(
    nc: bass.Bass,
    x: bass.AP,
    ctx: bass.AP,
    ctx_t: bass.AP,
    mask: bass.AP,
    gate_t: bass.AP,
    w13: bass.AP,
    w2ab: bass.AP,
    w2c: bass.AP,
    total: bass.AP,
):
    F32 = mybir.dt.float32
    F32R = mybir.dt.float32r
    BF16 = mybir.dt.bfloat16
    I32 = mybir.dt.int32
    U32 = mybir.dt.uint32
    U8 = mybir.dt.uint8
    ALU = mybir.AluOpType
    ACT = mybir.ActivationFunctionType
    AX = mybir.AxisListType

    P = 128
    B, S, D = x.shape
    M = ctx.shape[1]
    E = gate_t.shape[2]
    UNITS = w13.shape[0]
    I = w13.shape[3] // 2
    KD = D // P
    SHARED = UNITS - E
    K = 6
    CAP = 128
    N = B * S
    SCALE = float(D) ** -0.5
    EPS = 1e-5
    BIG = 1e30
    HUGE = 3.0e38
    IC = [(0, P), (P, P), (2 * P, I - 2 * P)]
    RAW = 4
    JOBS = E + B
    TURN = 10
    TURNS = JOBS // TURN
    RING = 5
    assert S == P and M == P and CAP == P and SHARED == 2 and E == 4 * B and JOBS % TURN == 0

    es = ExitStack()
    with es:
        def sb(name, shape, dt=F32):
            return es.enter_context(nc.sbuf_tensor(name, shape, dt))

        def bank(name):
            return es.enter_context(nc.psum_tensor(name, [P, 512], F32))

        def sem(name):
            return es.enter_context(nc.semaphore(name))

        tokens = nc.dram_tensor("tokens", [N + CAP, D], F32, kind="Internal").ap()
        tokens_t = nc.dram_tensor("tokens_t", [B, P, D], F32, kind="Internal").ap()
        table = nc.dram_tensor("slot_table", [CAP * E, 2], I32, kind="Internal").ap()

        def weights(tag):
            return (sb(f"w13h_{tag}", [P, KD * 2 * I], F32R), sb(f"w13l_{tag}", [P, KD * 2 * I], F32R),
                    sb(f"w2h_{tag}", [P, 3 * D], F32R), sb(f"w2l_{tag}", [P, 3 * D], F32R))

        ident = sb("ident", [P, P])
        before = sb("before", [P, P], BF16)
        ones = sb("ones", [P, P], BF16)
        valid = sb("valid", [P, B])
        mhalf = sb("mhalf", [P, 1])
        eio_i = sb("eio_i", [P, E], I32)
        eio = sb("eio", [P, E])
        ids = sb("ids", [P, B], I32)

        raw13 = [sb(f"raw13_{r}", [P, KD * 2 * I]) for r in range(RAW)]
        raw2 = [sb(f"raw2_{r}", [P, 3 * D]) for r in range(RAW)]
        x_in = [sb(f"x_in{p}", [P, D]) for p in range(2)]
        c_in = [sb(f"c_in{p}", [P, D]) for p in range(2)]
        xe = [*x_in, *c_in, sb("xe4", [P, D])]
        tTh = sb("tTh", [P, D], F32R)
        tTl = sb("tTl", [P, D], F32R)
        act = sb("act", [P, I])
        h = sb("h", [P, I])
        hTh = sb("hTh", [P, 3 * P], F32R)
        hTl = sb("hTl", [P, 3 * P], F32R)
        y = [sb(f"y{p}", [P, D]) for p in range(2)]
        tabs = sb("tabs", [P, E, 2], I32)
        from5 = sb("from5", [P, RING], I32)
        to5 = sb("to5", [P, RING], I32)
        gate5 = sb("gate5", [P, RING])

        st1 = sb("st1", [P, 6])
        ag1 = sb("ag1", [P, 2])
        ve1 = sb("ve1", [P, 1])
        rs1 = sb("rs1", [P, 1])
        mr1 = sb("mr1", [P, 1])
        mr2 = sb("mr2", [P, 1])
        vmax = sb("vmax", [P, B])
        smin = sb("smin", [P, 1])
        rsum = sb("rsum", [P, 1])
        rinv = sb("rinv", [P, 1])
        rval = sb("rval", [P, 1])
        st2 = sb("st2", [P, 6])
        ag2 = sb("ag2", [P, 2])
        ve2 = sb("ve2", [P, 1])
        rs2 = sb("rs2", [P, 1])
        top8 = sb("top8", [P, 8])
        idx8 = sb("idx8", [P, 8], U32)
        ntop = sb("ntop", [P, 1])
        etop = sb("etop", [P, 8])
        elog = sb("elog", [P, E])
        esum = sb("esum", [P, 1])
        einv = sb("einv", [P, 1])
        posx = sb("posx", [P, E])
        taken = sb("taken", [P, E])
        slot = [sb(f"slot{p}", [P, K], I32) for p in range(2)]
        vals = [sb(f"vals{p}", [P, K, 2], I32) for p in range(2)]
        gated = sb("gated", [P, I])

        x2_more = [sb(f"x2_{u}", [P, D]) for u in (2, 3)]

        w_stay = weights("stay")
        w_odd = weights("odd")

        with ExitStack() as es_a:
            def sba(name, shape, dt=F32):
                return es_a.enter_context(nc.sbuf_tensor(name, shape, dt))

            maskall = sba("maskall", [P, B, M])
            maskb = sba("maskb", [P, B * M], U8)
            ct_in = [sba(f"ct_in{p}", [P, D]) for p in range(2)]
            x2n = [sba(f"x2n_{p}", [P, D]) for p in range(2)]
            xn = sba("xn", [P, D])
            xnT = sba("xnT", [P, D])
            maskn = sba("maskn", [P, M])
            x2 = [sba(f"x2_{p}", [P, D]) for p in range(2)] + x2_more
            sn = sba("sn", [P, M])
            pr = sba("pr", [P, M])
            pT = sba("pT", [P, P])
            graw = sba("graw", [P, KD * E])
            tT = sba("tT", [P, D])
            dflt = sba("dflt", [P, E, 2], I32)
            oh = sba("oh", [P, K, E], BF16)
            ohp = sba("ohp", [P, K, E])
        w_even = weights("even")
        w_by = [w_even, w_odd]
        zeros = xe[4]

        UP = [[bank(f"up1_{p}"), bank(f"up3_{p}")] for p in range(2)]
        HT = bank("hT_ps")
        YB = bank("y_ps")
        TB = bank("tT_ps")
        AT = bank("attention_ps")
        LG, BE, ALL = TB[:, 0:E], TB[:, E:2 * E], TB[:, 2 * E:3 * E]

        const_step = sem("const_step")
        const_ready = sem("const_ready")
        mask_in = sem("mask_in")
        gate_in = sem("gate_in")
        mask_ready = sem("mask_ready")
        maskn_ready = sem("maskn_ready")
        tT_ready = sem("tT_ready")
        x_ld = [sem(f"x_ld{p}") for p in range(2)]
        c_ld = [sem(f"c_ld{p}") for p in range(2)]
        raw13_in = [[sem(f"raw13_in{r}_{a}") for a in range(2)] for r in range(RAW)]
        raw2_in = [sem(f"raw2_in{r}") for r in range(RAW)]
        wh13 = sem("wh13")
        wl13 = sem("wl13")
        wh2 = sem("wh2")
        wl2 = sem("wl2")
        wl2_pool = sem("wl2_pool")
        ln1_link = sem("ln1_link")
        var1_ready = sem("var1_ready")
        pow1_link = sem("pow1_link")
        pow2_link = sem("pow2_link")
        rstd1_ready = sem("rstd1_ready")
        xn_ready = sem("xn_ready")
        xnT_done = sem("xnT_done")
        xnT_ready = sem("xnT_ready")
        scores_done = sem("scores_done")
        soft_ready = sem("soft_ready")
        probs_ready = sem("probs_ready")
        pT_done = sem("pT_done")
        pT_ready = sem("pT_ready")
        read_done = sem("read_done")
        x2_ready = sem("x2_ready")
        ln2_link = sem("ln2_link")
        var2_ready = sem("var2_ready")
        rstd2_ready = sem("rstd2_ready")
        x2n_ready = sem("x2n_ready")
        tT_done = sem("tT_done")
        tTh_ready = sem("tTh_ready")
        tTl_ready = sem("tTl_ready")
        logits_done = sem("logits_done")
        top_link = sem("top_link")
        top_ready = sem("top_ready")
        etop_ready = sem("etop_ready")
        oh_ready = sem("oh_ready")
        pos_done = sem("pos_done")
        pos_read = sem("pos_read")
        slot_link = sem("slot_link")
        vals_ready = sem("vals_ready")
        table_init = sem("table_init")
        rows_init = sem("rows_init")
        table_st = [sem(f"table_st{p}") for p in range(2)]
        up_done = sem("up_done")
        tanh_ready = sem("tanh_ready")
        gated_link = sem("gated_link")
        h_ready = sem("h_ready")
        hT_done = sem("hT_done")
        hTh_ready = sem("hTh_ready")
        hTl_ready = sem("hTl_ready")
        down_done = sem("down_done")
        sum_ready = sem("sum_ready")
        tok_st = [sem(f"tok_st{p}") for p in range(2)]
        tT_st = sem("tT_st")
        sum_st = [sem(f"sum_st{p}") for p in range(2)]
        table_in = sem("table_in")
        from_link = sem("from_link")
        gate_link = sem("gate_link")
        gates_ready = sem("gates_ready")
        xe_in = [sem(f"xe_in{q}") for q in range(RING)]
        rows_ld = [sem(f"rows_ld{n}") for n in range(2)]
        bxT_done = sem("bxT_done")
        bxTh_ready = sem("bxTh_ready")
        bxTl_ready = sem("bxTl_ready")
        bup_done = sem("bup_done")
        bsilu_ready = sem("bsilu_ready")
        bh_ready = sem("bh_ready")
        bhT_done = sem("bhT_done")
        bhTh_ready = sem("bhTh_ready")
        bhTl_ready = sem("bhTl_ready")
        bdown_done = sem("bdown_done")
        by_ready = sem("by_ready")
        added = sem("added")

        block = es.enter_context(nc.Block())

        def even_odd(eng, first, pairs, step):
            with eng.Fori(0, pairs) as g:
                for j in range(2):
                    step(g * 2 + (first + j), (first + j) % 2, g + (first + j) // 2)

        class Job:

            def __init__(self, g, i):
                if i >= TURN or i < 0 and not (isinstance(g, int) and g == 0):
                    g, i = g + i // TURN, i % TURN
                self.last_turn = isinstance(g, int) and g == TURNS - 1
                at = i + 1
                self.n = g * TURN + at
                self.q = at % RING
                self.q_use = g * 2 + at // RING
                self.p = at % 2
                chunks = 1 if self.last_turn else i // 5 + 1
                self.expert = i >= 0 and (i > 0 if self.last_turn else i % 5 > 0)
                if self.expert:
                    ie = i - chunks
                    self.e = g * 8 + ie
                    self.r = (ie + 2) % RAW
                    self.r_use = g * 2 + (ie + 2) // RAW
                    self.w = w_by[ie % 2]
                    behind_chunk = i <= 2 if self.last_turn else i % 5 <= 2
                    self.w_freed = self.n - (2 if behind_chunk else 1)
                else:
                    self.chunk = g * 2 + (i // 5 + 1)
                    self.w = w_stay

        def by_turns(eng, step):
            for i in range(-1, TURN):
                step(0, i)
            with eng.Fori(1, TURNS - 1) as g:
                for i in range(TURN):
                    step(g, i)
            for i in range(TURN - 1):
                step(TURNS - 1, i)

        end = Job(TURNS - 1, TURN - 2)

        def rows_are_in(eng, j):
            if after(j.n, 2):
                eng.wait_ge(xe_in[j.q], j.q_use * 16 + (16 if j.q >= 2 else 0))
            else:
                eng.wait_ge(rows_ld[j.n], 16)

        def after(n, least):
            return not isinstance(n, int) or n >= least

        def by_four(eng, first, fours, step):
            with eng.Fori(0, fours) as g:
                for j in range(4):
                    step(g * 4 + (first + j), (first + j) % 2, g * 2 + (first + j) // 2, (first + j) % 4)

        def settled(eng):
            eng.nop(nofuse=True)

        @block.sync
        def _(sp):
            def load_chunk(c, p):
                sp.dma_start(x_in[p][:, :], x[c]).then_inc(x_ld[p], 16)
                sp.dma_start(ct_in[p][:, :].rearrange("p (k m) -> p k m", k=KD), ctx_t[c]).then_inc(c_ld[p], 16)
                sp.dma_start(c_in[p][:, :], ctx[c]).then_inc(c_ld[p], 16)

            def load_unit13(w, r, halves=(0, 1)):
                n = KD // 2
                for a in halves:
                    sp.dma_start(raw13[r][:, a * n * 2 * I:(a + 1) * n * 2 * I].rearrange("p (k i) -> p k i", k=n),
                                 w13[w][:, a * n:(a + 1) * n, :]).then_inc(raw13_in[r][a], 16)

            def load_unit2(w, r):
                sp.dma_start(raw2[r][:, 0:2 * D].rearrange("p (c n) -> p c n", c=2), w2ab[w]).then_inc(raw2_in[r], 16)
                sp.dma_start(raw2[r][0:IC[2][1], 2 * D:3 * D], w2c[w]).then_inc(raw2_in[r], 16)

            def reload_unit(w, r, use):
                r1, use1 = (r - 1) % RAW, use - (r == 0)
                sp.wait_ge(wl13, w * 2 - 6)
                settled(sp)
                sp.wait_ge(raw13_in[r1][1], use1 * 16 + 16)
                settled(sp)
                load_unit13(w, r, (0,))
                sp.wait_ge(raw2_in[r1], use1 * 32 + 32)
                settled(sp)
                load_unit13(w, r, (1,))
                if after(w, RAW + SHARED):
                    sp.wait_ge(wl2, w - RAW + 1 + SHARED)
                    settled(sp)
                    sp.wait_ge(wl2_pool, w - RAW + 1 - SHARED)
                    settled(sp)
                else:
                    sp.wait_ge(wl2, w * 2 - 6)
                    settled(sp)
                sp.wait_ge(raw13_in[r][0], use * 16 + 16)
                settled(sp)
                load_unit2(w, r)

            def store_total(c, p):
                sp.wait_ge(sum_ready, c + 1)
                sp.dma_start(total[bass.ds(c * P, P), :], y[p][:, :]).then_inc(sum_st[p], 16)

            def step(c, p, half, load=True):
                if after(c, 3):
                    store_total(c - 3, 1 - p)
                if load:
                    sp.wait_ge(x2_ready, c + 1)
                    load_chunk(c + 2, p)
                sp.wait_ge(x2n_ready, c + 1)
                sp.dma_start(tokens[bass.ds(c * P, P), :], x2n[p][:, :]).then_inc(tok_st[p], 16)
                sp.wait_ge(tT_ready, c + 1)
                sp.dma_start(tokens_t[c], tT[:, :]).then_inc(tT_st, 16)

            def load_job_rows(n):
                sp.wait_ge(tT_st, 16 * (B - 1 + n))
                sp.wait_ge(x2_ready, B - 1 + n)
                sp.dma_start(xe[n][:, :], tokens_t[n]).then_inc(rows_ld[n], 16)

            for p in range(2):
                sp.sem_inc(sum_st[p], 16)
            load_chunk(0, 0)
            sp.dma_start(maskb[:, :], mask.rearrange("b m -> (b m)").partition_broadcast(P)).then_inc(mask_in, 16)
            load_chunk(1, 1)
            load_unit13(0, 0)
            sp.dma_start(graw[:, :].rearrange("p (k e) -> p k e", k=KD), gate_t).then_inc(gate_in, 16)
            load_unit2(0, 0)
            step(0, 0, 0)
            for c in range(1, RAW):
                load_unit13(c, c)
                load_unit2(c, c)
                step(c, c % 2, c // 2)
            reload_unit(4, 0, 1)
            even_odd(sp, 4, (B - 6) // 2, step)
            step(B - 2, 0, B // 2 - 1, load=False)
            load_job_rows(0)
            step(B - 1, 1, B // 2 - 1, load=False)
            load_job_rows(1)
            store_total(B - 3, 1)
            store_total(B - 2, 0)
            store_total(B - 1, 1)
            sp.wait_ge(xe_in[2], 16)
            reload_unit(5, 1, 1)
            assert (UNITS - 6) % RAW == 0
            with sp.Fori(0, (UNITS - 6) // RAW) as g:
                for j in range(RAW):
                    reload_unit(g * RAW + (6 + j), (6 + j) % RAW, g + (6 + j) // RAW)
            sp.wait_ge(added, 16 * JOBS)

        @block.gpsimd
        def _(pool):
            n = [0]

            def made(ins):
                n[0] += 1
                ins.then_inc(const_step, 1)

            made(pool.memset(ident[:, :], 0.0))
            made(pool.memset(before[:, :], 1.0))
            made(pool.memset(ones[:, :], 1.0))
            made(pool.memset(zeros[:, :], 0.0))
            made(pool.memset(mhalf[:, :], -0.5))
            made(pool.memset(dflt[:, :, :], 0))
            made(pool.iota(eio_i[:, :], pattern=[[1, E]], base=0, channel_multiplier=0))
            made(pool.iota(ids[:, :], pattern=[[P, B]], base=0, channel_multiplier=1))
            pool.wait_ge(const_step, n[0])
            made(pool.affine_select(out=ident[:, :], in_=ident[:, :], compare_op=ALU.not_equal, fill=1.0,
                                    base=0, pattern=[[-1, P]], channel_multiplier=1))
            made(pool.affine_select(out=before[:, :], in_=before[:, :], compare_op=ALU.is_gt, fill=0.0,
                                    base=0, pattern=[[1, P]], channel_multiplier=-1))
            made(pool.iota(dflt[:, :, 0], pattern=[[0, E]], base=N, channel_multiplier=1))
            pool.wait_ge(const_step, n[0])
            pool.sem_inc(const_ready, 1)

            def rstd(c, var_ready, ve, rs, ready):
                pool.wait_ge(var_ready, c + 1)
                pool.tensor_tensor(rs[:, :], ve[:, :], mhalf[:, :], ALU.pow).then_inc(ready, 1)

            def rstd1(c):
                rstd(c, var1_ready, ve1, rs1, pow1_link)
                pool.wait_ge(pow1_link, c + 1)
                settled(pool)
                pool.tensor_scalar(mr1[:, :], ag1[:, 0:1], rs1[:, 0:1], -1.0, ALU.mult,
                                   ALU.mult).then_inc(rstd1_ready, 1)

            def rstd2(c):
                rstd(c, var2_ready, ve2, rs2, pow2_link)
                pool.wait_ge(pow2_link, c + 1)
                settled(pool)
                pool.tensor_scalar(mr2[:, :], ag2[:, 0:1], rs2[:, 0:1], -1.0, ALU.mult,
                                   ALU.mult).then_inc(rstd2_ready, 1)

            def slots(p, first, last):
                for k in range(first, last):
                    pool.indirect_dma_start(
                        out=table[:, :], out_offset=bass.IndirectOffsetOnAxis(ap=slot[p][:, k:k + 1], axis=0),
                        in_=vals[p][:, k, :], in_offset=None,
                        bounds_check=CAP * E - 1, oob_is_err=False).then_inc(table_st[p], 16)

            def slots_store(s, p, between=lambda: None):
                pool.wait_ge(vals_ready, s + 1)
                settled(pool)
                slots(p, 0, K // 2)
                between()
                slots(p, K // 2, K)

            def step(c, p, half, ahead=True):
                rstd2(c)
                slots_store(c - 1, 1 - p, between=(lambda: rstd1(c + 2)) if ahead else (lambda: None))

            rstd1(0)
            pool.dma_start(table.rearrange("(p e) two -> p (e two)", p=P),
                           dflt[:, :, :].rearrange("p e two -> p (e two)")).then_inc(table_init, 16)
            pool.dma_start(tokens[N:N + CAP, :], zeros[:, :]).then_inc(rows_init, 16)
            pool.dma_start(total[N:N + CAP, :], zeros[:, :]).then_inc(rows_init, 16)
            rstd1(1)
            rstd2(0)
            rstd1(2)
            pool.wait_ge(table_init, 16)
            even_odd(pool, 1, (B - 4) // 2, step)
            step(B - 3, 1, B // 2 - 2)
            step(B - 2, 0, B // 2 - 1, ahead=False)

            def rows_of(j, into, link):
                src = tabs[:, bass.ds(j.e, 1), 0] if j.expert else ids[:, bass.ds(j.chunk, 1)]
                pool.tensor_copy(into[:, j.q:j.q + 1], src).then_inc(link, 1)

            def gather(j):
                if not j.expert:
                    pool.dma_start(xe[j.q][:, :], tokens_t[j.chunk]).then_inc(xe_in[j.q], 16)
                    return
                rows_of(j, from5, from_link)
                pool.wait_ge(from_link, j.e + 1)
                settled(pool)
                pool.indirect_dma_start(
                    out=xe[j.q][:, :], out_offset=None, in_=tokens[:, :],
                    in_offset=bass.IndirectOffsetOnAxis(ap=from5[:, j.q:j.q + 1], axis=0),
                    bounds_check=N + CAP - 1, oob_is_err=True).then_inc(xe_in[j.q], 16)

            def slots_of(j):
                rows_of(j, to5, gate_link)
                if j.expert:
                    ins = pool.tensor_copy(gate5[:, j.q:j.q + 1], tabs[:, bass.ds(j.e, 1), 1].bitcast(F32))
                else:
                    ins = pool.memset(gate5[:, j.q:j.q + 1], 1.0)
                ins.then_inc(gates_ready, 1)

            def scatter(j):
                pool.wait_ge(gate_link, j.n + 1)
                pool.wait_ge(by_ready, j.n + 1)
                settled(pool)
                pool.indirect_dma_start(
                    out=total[:, :], out_offset=bass.IndirectOffsetOnAxis(ap=to5[:, j.q:j.q + 1], axis=0),
                    in_=y[j.p][:, :], in_offset=None,
                    bounds_check=N + CAP - 1, oob_is_err=True, compute_op=ALU.add).then_inc(added, 16)

            rstd2(B - 1)
            slots_store(B - 2, 0)
            slots_store(B - 1, 1)
            for p in range(2):
                pool.wait_ge(table_st[p], 16 * K * B // 2)
            pool.dma_start(tabs[:, :, :].rearrange("p e two -> p (e two)"),
                           table.rearrange("(p e) two -> p (e two)", p=P)).then_inc(table_in, 16)
            pool.wait_ge(rows_init, 32)
            pool.wait_ge(x2_ready, B)
            pool.wait_ge(tT_st, 16 * B)
            for p in range(2):
                pool.wait_ge(tok_st[p], 16 * B // 2)
            slots_of(Job(0, -1))
            slots_of(Job(0, 0))
            pool.wait_ge(table_in, 16)
            for i in range(1, RING - 1):
                gather(Job(0, i))

            def split2_rest(j):
                n = IC[2][1]
                pool.wait_ge(wh2, (j.e + 2) * 2 + 2)
                settled(pool)
                pool.tensor_tensor(j.w[3][0:n, 2 * D:3 * D], raw2[j.r][0:n, 2 * D:3 * D],
                                   j.w[2][0:n, 2 * D:3 * D].bitcast(F32), ALU.subtract).then_inc(wl2_pool, 1)

            def job(g, i):
                j = Job(g, i)
                last_turn = isinstance(g, int) and g == TURNS - 1
                if after(j.n, 1) and Job(g, i - 1).expert:
                    split2_rest(Job(g, i - 1))
                if after(j.n, 2):
                    if after(j.n, 3):
                        pool.wait_ge(added, (j.n - 2) * 16)
                    else:
                        for p in range(2):
                            pool.wait_ge(sum_st[p], 16 * B // 2 + 16)
                    scatter(Job(g, i - 2))
                if last_turn and i == TURN - 2:
                    split2_rest(j)
                if not (last_turn and i + RING >= TURN - 1):
                    if j.expert:
                        pool.wait_ge(bxT_done, j.e + 1)
                    else:
                        pool.wait_ge(bxTl_ready, j.n + 1)
                    settled(pool)
                    gather(Job(g, i + RING))
                if not (last_turn and i + 2 >= TURN - 1):
                    slots_of(Job(g, i + 2))

            by_turns(pool, job)
            for j in (Job(TURNS - 1, TURN - 3), end):
                pool.wait_ge(added, 16 * j.n)
                scatter(j)
            pool.wait_ge(added, 16 * JOBS)

        @block.scalar
        def _(ac):
            def split13(w, r, use, halves=(0, 1)):
                n = KD * I
                for a in halves:
                    ac.wait_ge(raw13_in[r][a], use * 16 + 16)
                    ac.activation(w[0][:, a * n:(a + 1) * n], raw13[r][:, a * n:(a + 1) * n],
                                  ACT.Copy).then_inc(wh13, 1)

            def split2(w, r, use, parts=(0, 1)):
                ac.wait_ge(raw2_in[r], use * 32 + 32)
                for a, (rows, lo, hi) in enumerate(((P, 0, 2 * D), (IC[2][1], 2 * D, 3 * D))):
                    if a in parts:
                        ac.activation(w[2][0:rows, lo:hi], raw2[r][0:rows, lo:hi], ACT.Copy).then_inc(wh2, 1)

            def hi_of_hT(done, at, freed, free_at, ready):
                ac.wait_ge(done, at)
                if free_at is not None:
                    ac.wait_ge(freed, free_at)
                ac.activation(hTh[:, 0:2 * P], HT[:, 0:2 * P], ACT.Copy)
                ac.activation(hTh[0:IC[2][1], 2 * P:3 * P], HT[0:IC[2][1], 2 * P:3 * P], ACT.Copy).then_inc(ready, 1)

            def tanh(s, p):
                ac.wait_ge(up_done, s + 1)
                if after(s, 1):
                    ac.wait_ge(gated_link, s)
                ac.activation(act[:, :], UP[p][0][:, 0:I], ACT.Tanh, scale=0.5).then_inc(tanh_ready, 1)

            def shared_hT(s):
                hi_of_hT(hT_done, s + 1, down_done, s if after(s, 1) else None, hTh_ready)

            def copy_xnT(c, first=False):
                ac.wait_ge(xnT_done, c + 1)
                if not first:
                    ac.wait_ge(scores_done, c)
                ac.activation(xnT[:, :], AT[:, :], ACT.Copy).then_inc(xnT_ready, 1)

            def norm1_apply(c, p):
                ac.wait_ge(rstd1_ready, c + 1)
                if after(c, 1):
                    ac.wait_ge(xnT_done, c)
                ac.activation(xn[:, :], x_in[p][:, :], ACT.Identity, bias=mr1[:, 0:1],
                              scale=rs1[:, 0:1]).then_inc(xn_ready, 1)

            def probs(c):
                ac.wait_ge(soft_ready, c + 1)
                if after(c, 1):
                    ac.wait_ge(pT_done, c)
                ac.activation(pr[:, :], sn[:, :], ACT.Exp, bias=smin[:, :], scale=-1.0,
                              accum_out=rsum[:, :]).then_inc(probs_ready, 1)

            def norm2_apply(c, p, half, u):
                ac.wait_ge(rstd2_ready, c + 1)
                if after(c, 2):
                    ac.wait_ge(tok_st[p], half * 16)
                ac.activation(x2n[p][:, :], x2[u][:, :], ACT.Identity, bias=mr2[:, 0:1],
                              scale=rs2[:, 0:1]).then_inc(x2n_ready, 1)

            def mask_of(c):
                if after(c, 1):
                    ac.wait_ge(soft_ready, c)
                ac.activation(maskn[:, :], maskall[:, bass.ds(c, 1), :].squeeze(1), ACT.Copy).then_inc(maskn_ready, 1)

            def step(c, p, half, u, attend=True, shared=True, ahead=True, between=lambda: None):
                s = c - 1
                if after(s, 1):
                    shared_hT(s - 1)
                if attend:
                    ac.wait_ge(pT_done, c + 1)
                    if after(c, 1):
                        ac.wait_ge(read_done, c)
                    ac.activation(pT[:, :], AT[:, M:2 * M], ACT.Copy).then_inc(pT_ready, 1)
                if shared:
                    ac.wait_ge(top_ready, s + 1)
                    if after(s, 1):
                        ac.wait_ge(vals_ready, s)
                    ac.activation(elog[:, :], LG, ACT.Exp, bias=ntop[:, :], accum_out=esum[:, :])
                    ac.activation(etop[:, :], top8[:, :], ACT.Exp, bias=ntop[:, :]).then_inc(etop_ready, 1)
                if ahead:
                    norm1_apply(c + 1, 1 - p)
                    mask_of(c + 1)
                between()
                if ahead:
                    copy_xnT(c + 1)
                if attend:
                    norm2_apply(c, p, half, u)
                if shared:
                    tanh(s, 1 - p)
                if attend:
                    ac.wait_ge(tT_done, c + 1)
                    if after(c, 1):
                        ac.wait_ge(logits_done, c)
                        ac.wait_ge(tT_st, c * 16)
                    ac.activation(tT[:, :], TB[:, :], ACT.Copy).then_inc(tT_ready, 1)
                    ac.wait_ge(tT_ready, c + 1)
                    ac.activation(tTh[:, :], tT[:, :], ACT.Copy).then_inc(tTh_ready, 1)
                if ahead:
                    probs(c + 1)

            norm1_apply(0, 0)
            copy_xnT(0, first=True)
            ac.wait_ge(mask_ready, 1)
            mask_of(0)
            probs(0)
            step(0, 0, 0, 0, shared=False, between=lambda: split13(w_odd, 0, 0))
            step(1, 1, 0, 1, between=lambda: split2(w_odd, 0, 0))
            step(2, 0, 1, 2)
            by_four(ac, 3, B // 4 - 2, step)
            step(B - 5, 1, B // 2 - 3, 3, between=lambda: split13(w_stay, 1, 0, halves=(0,)))
            step(B - 4, 0, B // 2 - 2, 0, between=lambda: split13(w_stay, 1, 0, halves=(1,)))
            step(B - 3, 1, B // 2 - 2, 1, between=lambda: split2(w_stay, 1, 0))
            step(B - 2, 0, B // 2 - 1, 2)
            step(B - 1, 1, B // 2 - 1, 3, ahead=False)
            step(B, 0, B // 2, 0, attend=False, ahead=False)

            def silu(j):
                ac.wait_ge(bup_done, j.n + 1)
                if after(j.n, 1):
                    ac.wait_ge(bh_ready, j.n)
                ac.activation(act[:, :], UP[j.p][0][:, 0:I], ACT.Silu).then_inc(bsilu_ready, 1)

            def hi_of_x(j):
                if j.expert:
                    ac.wait_ge(bxT_done, j.e + 1)
                else:
                    rows_are_in(ac, j)
                if after(j.n, 1):
                    ac.wait_ge(bup_done, j.n)
                ac.activation(tTh[:, :], (TB if j.expert else xe[j.q])[:, :], ACT.Copy).then_inc(bxTh_ready, 1)

            def weigh(j):
                ac.wait_ge(bdown_done, j.n + 1)
                ac.wait_ge(gates_ready, j.n + 1)
                if after(j.n, 2):
                    ac.wait_ge(added, (j.n - 1) * 16)
                else:
                    ac.wait_ge(sum_st[j.p], 16 * B // 2 + 16)
                ac.activation(y[j.p][:, :], YB[:, :], ACT.Copy, scale=gate5[:, j.q:j.q + 1]).then_inc(by_ready, 1)

            def split13_of(j, halves):
                if 0 in halves:
                    if after(j.e, 2):
                        ac.wait_ge(bup_done, j.w_freed)
                    elif j.e == 1:
                        ac.wait_ge(up_done, B)
                    else:
                        ac.wait_ge(tT_done, B)
                        for p in range(2):
                            ac.wait_ge(tok_st[p], 16 * B // 2)
                split13(j.w, j.r, j.r_use, halves)

            def split2_begin(j):
                if after(j.e, 2):
                    ac.wait_ge(bdown_done, j.w_freed)
                elif j.e == 1:
                    ac.wait_ge(down_done, B)
                else:
                    ac.wait_ge(sum_ready, B)
                    ac.wait_ge(vals_ready, B)
                    ac.wait_ge(table_init, 16)
                    ac.wait_ge(tT_st, 16 * B)
                split2(j.w, j.r, j.r_use, parts=(0,))

            def split2_end(j):
                split2(j.w, j.r, j.r_use, parts=(1,))

            def job(g, i):
                j = Job(g, i)
                prev = Job(g, i - 1) if after(j.n, 1) else None
                nxt = Job(g, i + 1)
                first = isinstance(g, int) and j.n == 0
                last = isinstance(g, int) and j.n == JOBS - 1
                if not first:
                    hi_of_hT(bhT_done, j.n, bdown_done if after(j.n, 2) else down_done,
                             j.n - 1 if after(j.n, 2) else B, bhTh_ready)
                    if prev.expert:
                        split2_begin(prev)
                if not last and nxt.expert:
                    split13_of(nxt, (0,))
                if not first and prev.expert:
                    split2_end(prev)
                silu(j)
                if last:
                    split2_begin(j)
                    split2_end(j)
                if not last:
                    hi_of_x(nxt)
                    if nxt.expert:
                        split13_of(nxt, (1,))
                if not first:
                    weigh(prev)

            hi_of_x(Job(0, -1))
            shared_hT(B - 1)
            by_turns(ac, job)
            hi_of_hT(bhT_done, JOBS, bdown_done, JOBS - 1, bhTh_ready)
            weigh(end)

        @block.vector
        def _(ve):
            class Links:

                def __init__(self, s, n, step):
                    self.s, self.n, self.base, self.k = s, n, step * n, 0

                def done(self, ins):
                    ins.then_inc(self.s, 1)
                    self.k += 1
                    assert self.k <= self.n

                def wait(self):
                    ve.wait_ge(self.s, self.base + self.k)

            def split13(w, r, at, halves=(0, 1)):
                n = KD * I
                for a in halves:
                    ve.wait_ge(wh13, at + (a + 1))
                    ve.tensor_tensor(w[1][:, a * n:(a + 1) * n], raw13[r][:, a * n:(a + 1) * n],
                                     w[0][:, a * n:(a + 1) * n].bitcast(F32), ALU.subtract).then_inc(wl13, 1)

            def split13_quarter(w, r, at, quarter):
                n = KD * I // 2
                part = slice(quarter * n, (quarter + 1) * n)
                ve.wait_ge(wh13, at + (quarter // 2 + 1))
                ins = ve.tensor_tensor(w[1][:, part], raw13[r][:, part], w[0][:, part].bitcast(F32), ALU.subtract)
                if quarter % 2 == 1:
                    ins.then_inc(wl13, 1)

            SPLIT2 = [(P, 0, 2 * D), (IC[2][1], 2 * D, 3 * D)]

            def split2(w, r, u, parts=(0, 1)):
                for a in parts:
                    rows, lo, hi = SPLIT2[a]
                    ve.wait_ge(wh2, u * 2 + (a + 1))
                    ve.tensor_tensor(w[3][0:rows, lo:hi], raw2[r][0:rows, lo:hi],
                                     w[2][0:rows, lo:hi].bitcast(F32), ALU.subtract).then_inc(wl2, 1)

            def lo_of_hT(hi_ready, at, ready):
                ve.wait_ge(hi_ready, at)
                ve.tensor_tensor(hTl[:, 0:2 * P], HT[:, 0:2 * P], hTh[:, 0:2 * P].bitcast(F32), ALU.subtract)
                n = IC[2][1]
                ve.tensor_tensor(hTl[0:n, 2 * P:3 * P], HT[0:n, 2 * P:3 * P], hTh[0:n, 2 * P:3 * P].bitcast(F32),
                                 ALU.subtract).then_inc(ready, 1)

            def lo_of_x(src, hi_ready, at, ready):
                ve.wait_ge(hi_ready, at)
                ve.tensor_tensor(tTl[:, :], src[:, :], tTh[:, :].bitcast(F32), ALU.subtract).then_inc(ready, 1)

            def norm_stats(c, src, st, ag, vv, link, ready):
                ln = Links(link, 2, c)
                ln.done(ve.bn_stats(st[:, :], src))
                ln.wait()
                settled(ve)
                ln.done(ve.bn_aggr(ag[:, :], st[:, :]))
                ln.wait()
                ve.tensor_scalar(vv[:, :], ag[:, 1:2], EPS, None, ALU.add).then_inc(ready, 1)

            def norm1_stats(c, p, half):
                ve.wait_ge(x_ld[p], half * 16 + 16)
                if after(c, 1):
                    ve.wait_ge(xn_ready, c)
                norm_stats(c, x_in[p][:, :], st1, ag1, ve1, ln1_link, var1_ready)

            def route_top(s, c, attend):
                ve.wait_ge(logits_done, s + 1)
                settled(ve)
                ln = Links(top_link, 2, s)
                ln.done(ve.max(top8[:, :], LG))
                if attend:
                    softmax_inv(c)
                ln.wait()
                settled(ve)
                ln.done(ve.max_index(idx8[:, :], top8[:, :], LG))
                ve.tensor_scalar(ntop[:, :], top8[:, 0:1], -1.0, None, ALU.mult).then_inc(top_ready, 1)
                if attend:
                    softmax_valid(c)
                ln.wait()
                ve.tensor_tensor(oh[:, :, :], idx8[:, 0:K].unsqueeze(2).to_broadcast([P, K, E]),
                                 eio[:, :].unsqueeze(1).to_broadcast([P, K, E]), ALU.is_equal).then_inc(oh_ready, 1)

            def softmax_inv(c):
                ve.wait_ge(probs_ready, c + 1)
                ve.reciprocal(rinv[:, :], rsum[:, :]).then_inc(ln2_link, 1)

            def softmax_valid(c):
                ve.wait_ge(ln2_link, c * 4 + 1)
                ve.tensor_scalar(rval[:, :], rinv[:, :], valid[:, bass.ds(c, 1)], None,
                                 ALU.mult).then_inc(ln2_link, 1)

            def max_score(c):
                ve.wait_ge(scores_done, c + 1)
                ve.wait_ge(maskn_ready, c + 1)
                settled(ve)
                ve.tensor_tensor_reduce(out=sn[:, :], in0=AT[:, 0:M], in1=maskn[:, :],
                                        scale=-SCALE, scalar=HUGE, op0=ALU.add, op1=ALU.min,
                                        accum_out=smin[:, :]).then_inc(soft_ready, 1)

            def route_places(s):
                ve.wait_ge(pos_done, s + 1)
                if after(s, 1):
                    ve.wait_ge(pos_read, s * 2)
                ve.scalar_tensor_tensor(posx[:, :], BE, float(E), taken[:, :], ALU.mult,
                                        ALU.add).then_inc(pos_read, 1)

            def route_taken(s):
                ve.wait_ge(pos_read, s * 2 + 1)
                ve.scalar_tensor_tensor(taken[:, :], ALL, float(E), taken[:, :], ALU.mult,
                                        ALU.add).then_inc(pos_read, 1)
                ve.wait_ge(etop_ready, s + 1)
                ve.reciprocal(einv[:, :], esum[:, :]).then_inc(slot_link, 1)

            def route_ids(s, p, half):
                if after(s, 2):
                    ve.wait_ge(table_st[p], half * (16 * K))
                ve.tensor_copy(vals[p][:, :, 0], ids[:, bass.ds(s, 1)].to_broadcast([P, K]))

            def route_gates(s, p):
                ve.wait_ge(slot_link, s * 2 + 1)
                ve.tensor_scalar(vals[p][:, :, 1].bitcast(F32), etop[:, 0:K], einv[:, 0:1], None, ALU.mult)

            def route_picks(s):
                ve.wait_ge(pos_read, s * 2 + 2)
                ve.tensor_tensor(ohp[:, :, :], oh[:, :, :], posx[:, :].unsqueeze(1).to_broadcast([P, K, E]),
                                 ALU.mult).then_inc(slot_link, 1)

            def route_slots(s, p):
                ve.wait_ge(slot_link, s * 2 + 2)
                with nc.allow_low_precision(reason="whole numbers under 2 ** 24, one of each row's nonzero"):
                    ve.tensor_reduce(slot[p][:, :], ohp[:, :, :], AX.X, ALU.add).then_inc(vals_ready, 1)

            def gate_begin(s, p):
                ve.wait_ge(tanh_ready, s + 1)
                ve.scalar_tensor_tensor(gated[:, :], act[:, :], 1.0, UP[p][0][:, 0:I], ALU.add,
                                        ALU.mult).then_inc(gated_link, 1)

            def gate_end(s, p):
                if after(s, 1):
                    ve.wait_ge(hT_done, s)
                ve.wait_ge(gated_link, s + 1)
                ve.scalar_tensor_tensor(h[:, :], gated[:, :], 0.5, UP[p][1][:, 0:I], ALU.mult,
                                        ALU.mult).then_inc(h_ready, 1)

            def store_sum(s, p, half, u):
                ve.wait_ge(down_done, s + 1)
                ve.wait_ge(sum_st[p], half * 16 + 16)
                ve.tensor_tensor(y[p][:, :], YB[:, :], x2[u][:, :], ALU.add).then_inc(sum_ready, 1)

            def step(c, p, half, u, attend=True, shared=True, ahead=True, ahead2=True, between=lambda: None):
                s, ps = c - 1, 1 - p
                halfs = half - 1 + p
                if after(s, 2) and attend:
                    store_sum(s - 2, ps, halfs - 1, (u + 1) % 4)
                if shared:
                    route_top(s, c, attend)
                    if not attend:
                        store_sum(s - 2, ps, halfs - 1, (u + 1) % 4)
                    if after(s, 1):
                        lo_of_hT(hTh_ready, s, hTl_ready)
                else:
                    softmax_inv(c)
                    softmax_valid(c)
                if attend:
                    ve.wait_ge(read_done, c + 1)
                    ve.wait_ge(ln2_link, c * 4 + 2)
                    if after(c, 3):
                        ve.wait_ge(sum_ready, c - 2)
                    ve.scalar_tensor_tensor(x2[u][:, :], AT[:, :], rval[:, :], x_in[p][:, :], ALU.mult,
                                            ALU.add).then_inc(x2_ready, 1)
                if shared:
                    route_places(s)
                if attend:
                    ve.wait_ge(x2_ready, c + 1)
                    ve.bn_stats(st2[:, :], x2[u][:, :]).then_inc(ln2_link, 1)
                if shared:
                    route_taken(s)
                    route_ids(s, ps, halfs)
                if attend:
                    ve.wait_ge(ln2_link, c * 4 + 3)
                    settled(ve)
                    ve.bn_aggr(ag2[:, :], st2[:, :]).then_inc(ln2_link, 1)
                    if shared:
                        route_gates(s, ps)
                    ve.wait_ge(ln2_link, c * 4 + 4)
                    ve.tensor_scalar(ve2[:, :], ag2[:, 1:2], EPS, None, ALU.add).then_inc(var2_ready, 1)
                elif shared:
                    route_gates(s, ps)
                if shared:
                    route_picks(s)
                    route_slots(s, ps)
                between()
                if shared:
                    gate_begin(s, ps)
                if ahead:
                    max_score(c + 1)
                if shared:
                    gate_end(s, ps)
                if ahead2:
                    norm1_stats(c + 2, p, half + 1)
                if attend:
                    lo_of_x(tT, tTh_ready, c + 1, tTl_ready)

            norm1_stats(0, 0, 0)
            far = BIG / SCALE
            ve.wait_ge(mask_in, 16)
            ve.tensor_scalar(maskall[:, :, :].rearrange("p b m -> p (b m)"), maskb[:, :], far, -far, ALU.mult,
                             ALU.add).then_inc(mask_ready, 1)
            ve.wait_ge(mask_ready, 1)
            ve.tensor_reduce(vmax[:, :], maskall[:, :, :], AX.X, ALU.max).then_inc(mask_ready, 1)
            ve.wait_ge(const_ready, 1)
            ve.tensor_copy(eio[:, :], eio_i[:, :]).then_inc(mask_ready, 1)
            ve.tensor_copy(taken[:, :], eio_i[:, :]).then_inc(mask_ready, 1)
            ve.wait_ge(mask_ready, 4)
            ve.tensor_scalar(valid[:, :], vmax[:, :], 0.0, None, ALU.is_ge).then_inc(mask_ready, 1)
            ve.wait_ge(mask_ready, 5)
            max_score(0)
            norm1_stats(1, 1, 0)
            step(0, 0, 0, 0, shared=False, between=lambda: split13(w_odd, 0, 0))
            step(1, 1, 0, 1, between=lambda: split2(w_odd, 0, 0))
            step(2, 0, 1, 2)
            assert B % 4 == 0
            by_four(ve, 3, B // 4 - 2, step)
            step(B - 5, 1, B // 2 - 3, 3, between=lambda: split13_quarter(w_stay, 1, 2, 0))
            step(B - 4, 0, B // 2 - 2, 0, between=lambda: split13_quarter(w_stay, 1, 2, 1))
            step(B - 3, 1, B // 2 - 2, 1, between=lambda: split13_quarter(w_stay, 1, 2, 2))
            step(B - 2, 0, B // 2 - 1, 2, ahead2=False, between=lambda: split13_quarter(w_stay, 1, 2, 3))
            step(B - 1, 1, B // 2 - 1, 3, ahead=False, ahead2=False, between=lambda: split2(w_stay, 1, 1, parts=(1,)))
            step(B, 0, B // 2, 0, attend=False, ahead=False, ahead2=False)

            def gate(j):
                ve.wait_ge(bsilu_ready, j.n + 1)
                if after(j.n, 1):
                    ve.wait_ge(bhT_done, j.n)
                else:
                    ve.wait_ge(hT_done, B)
                ve.tensor_tensor(h[:, :], act[:, :], UP[j.p][1][:, 0:I], ALU.mult).then_inc(bh_ready, 1)

            def job(g, i):
                j, nxt = Job(g, i), Job(g, i + 1)
                first = isinstance(g, int) and j.n == 0
                last = isinstance(g, int) and j.n == JOBS - 1
                if not first:
                    lo_of_hT(bhTh_ready, j.n, bhTl_ready)
                    prev = Job(g, i - 1)
                    if prev.expert:
                        split2(prev.w, prev.r, prev.e + 2, parts=(0,))
                if not last and nxt.expert:
                    split13(nxt.w, nxt.r, (nxt.e + 2) * 2, halves=(0,))
                gate(j)
                if last:
                    split2(j.w, j.r, j.e + 2, parts=(0,))
                if not last:
                    lo_of_x(TB if nxt.expert else xe[nxt.q], bxTh_ready, j.n + 2, bxTl_ready)
                    if nxt.expert:
                        split13(nxt.w, nxt.r, (nxt.e + 2) * 2, halves=(1,))
                if first:
                    store_sum(B - 1, 1, B // 2 - 1, 3)

            lo_of_x(xe[0], bxTh_ready, 1, bxTl_ready)
            store_sum(B - 2, 0, B // 2 - 1, 2)
            lo_of_hT(hTh_ready, B, hTl_ready)
            split2(w_stay, 1, 1, parts=(0,))
            by_turns(ve, job)
            lo_of_hT(bhTh_ready, JOBS, bhTl_ready)

        @block.tensor
        def _(pe):
            def transpose4(dst, src):
                for k in range(KD):
                    last = pe.transpose(dst[:, k * P:(k + 1) * P], src[:, k * P:(k + 1) * P], ident[:, :])
                return last

            def transpose_h():
                for j, (lo, n) in enumerate(IC):
                    last = pe.transpose(HT[0:n, j * P:(j + 1) * P], h[:, lo:lo + n], ident[:, :])
                return last

            def up(w, banks, first=0, last=KD):
                for k in range(first, last):
                    for a, b in ((tTh, w[0]), (tTh, w[1]), (tTl, w[0])):
                        for v in range(2):
                            o = (2 * k + v) * I
                            ins = pe.matmul(banks[v][:, 0:I], a[:, k * P:(k + 1) * P], b[:, o:o + I],
                                            start=(k == 0 and a is tTh and b is w[0]),
                                            stop=(k == KD - 1 and a is tTl))
                return ins

            def down(w, first=0, last=len(IC)):
                for j in range(first, last):
                    n = IC[j][1]
                    for a, b in ((hTh, w[2]), (hTh, w[3]), (hTl, w[2])):
                        ins = pe.matmul(YB[:, :], a[0:n, j * P:(j + 1) * P], b[0:n, j * D:(j + 1) * D],
                                        start=(j == 0 and a is hTh and b is w[2]),
                                        stop=(j == 2 and a is hTl))
                return ins

            def count(dst, sel):
                for k in range(K):
                    last = pe.matmul(dst, sel[:, :], oh[:, k, :], start=(k == 0), stop=(k == K - 1))
                return last

            def shared_hT(s):
                pe.wait_ge(h_ready, s + 1)
                if after(s, 1):
                    pe.wait_ge(hTl_ready, s)
                transpose_h().then_inc(hT_done, 1)

            def shared_down_begin(s):
                pe.wait_ge(hTl_ready, s + 1)
                if after(s, 1):
                    pe.wait_ge(sum_ready, s)
                else:
                    pe.wait_ge(wl2, 2)
                down(w_odd, 0, 1)

            def shared_down_end(s):
                down(w_odd, 2, 3).then_inc(down_done, 1)

            def transpose_xn(c):
                pe.wait_ge(xn_ready, c + 1)
                if after(c, 1):
                    pe.wait_ge(x2_ready, c)
                transpose4(AT, xn).then_inc(xnT_done, 1)

            def transpose_x(j):
                rows_are_in(pe, j)
                transpose4(TB, xe[j.q]).then_inc(bxT_done, 1)

            def scores(c, p, half):
                pe.wait_ge(xnT_ready, c + 1)
                pe.wait_ge(c_ld[p], half * 32 + 32)
                for k in range(KD):
                    last = pe.matmul(AT[:, 0:M], xnT[:, k * P:(k + 1) * P], ct_in[p][:, k * M:(k + 1) * M],
                                     start=(k == 0), stop=(k == KD - 1))
                last.then_inc(scores_done, 1)

            def step(c, p, half, attend=True, shared=True, ahead=True):
                s = c - 1
                if shared:
                    pe.wait_ge(tT_ready, s + 1)
                    for k in range(KD):
                        last = pe.matmul(LG, tT[:, k * P:(k + 1) * P], graw[:, k * E:(k + 1) * E],
                                         start=(k == 0), stop=(k == KD - 1))
                    last.then_inc(logits_done, 1)
                if not attend:
                    shared_hT(s - 1)
                if attend:
                    pe.wait_ge(probs_ready, c + 1)
                    pe.transpose(AT[:, M:2 * M], pr[:, :], ident[:, :]).then_inc(pT_done, 1)
                if shared:
                    if after(s, 2):
                        pe.wait_ge(h_ready, s - 1)
                    elif s == 0:
                        pe.wait_ge(wl13, 1)
                    pe.wait_ge(tTl_ready, s + 1)
                    up(w_odd, UP[1 - p], 0, 1)
                if attend:
                    pe.wait_ge(pT_ready, c + 1)
                    pe.matmul(AT[:, :], pT[:, :], c_in[p][:, :], start=True, stop=True).then_inc(read_done, 1)
                if shared:
                    pe.wait_ge(oh_ready, s + 1)
                    pe.wait_ge(etop_ready, s + 1)
                    count(BE, before)
                    count(ALL, ones).then_inc(pos_done, 1)
                    up(w_odd, UP[1 - p], 1, 2)
                if ahead:
                    transpose_xn(c + 1)
                if shared:
                    if not after(s, 1):
                        pe.wait_ge(wl13, 2)
                    up(w_odd, UP[1 - p], 2, 4).then_inc(up_done, 1)
                if ahead:
                    scores(c + 1, 1 - p, half + p)
                elif attend:
                    shared_down_begin(s - 1)
                    down(w_odd, 1, 2)
                if attend:
                    pe.wait_ge(x2n_ready, c + 1)
                    if shared:
                        pe.wait_ge(pos_read, s * 2 + 2)
                    transpose4(TB, x2n[p]).then_inc(tT_done, 1)
                if after(s, 1) and (ahead or not attend):
                    shared_down_begin(s - 1)
                    down(w_odd, 1, 2)
                if after(s, 1):
                    shared_down_end(s - 1)
                if shared and (ahead or not attend):
                    shared_hT(s)

            pe.wait_ge(const_ready, 1)
            transpose_xn(0)
            scores(0, 0, 0)
            step(0, 0, 0, shared=False)
            pe.wait_ge(gate_in, 16)
            step(1, 1, 0)
            step(2, 0, 1)
            even_odd(pe, 3, (B - 4) // 2, step)
            step(B - 1, 1, B // 2 - 1, ahead=False)
            step(B, 0, B // 2, attend=False, ahead=False)

            def job_up(j):
                pe.wait_ge(bxTl_ready, j.n + 1)
                if after(j.n, 2):
                    pe.wait_ge(bh_ready, j.n - 1)
                else:
                    pe.wait_ge(h_ready, B - 1 + j.n)
                if j.expert:
                    pe.wait_ge(wl13, (j.e + 2) * 2 + 1)
                up(j.w, UP[j.p], 0, KD // 2)
                if j.expert:
                    pe.wait_ge(wl13, (j.e + 2) * 2 + 2)
                up(j.w, UP[j.p], KD // 2, KD).then_inc(bup_done, 1)

            def job_down(j):
                pe.wait_ge(bhTl_ready, j.n + 1)
                if j.expert:
                    pe.wait_ge(wl2, j.e + 1 + 2 * SHARED)
                if after(j.n, 1):
                    pe.wait_ge(by_ready, j.n)
                else:
                    pe.wait_ge(sum_ready, B)
                    pe.wait_ge(wl2, 4)
                down(j.w, 0, 2)
                if j.expert:
                    pe.wait_ge(wl2_pool, j.e + 1)
                down(j.w, 2, 3).then_inc(bdown_done, 1)

            def job_hT(j):
                pe.wait_ge(bh_ready, j.n + 1)
                transpose_h().then_inc(bhT_done, 1)

            def job(g, i):
                j, nxt = Job(g, i), Job(g, i + 1)
                job_up(j)
                if not (isinstance(g, int) and j.n == JOBS - 1) and nxt.expert:
                    if isinstance(g, int) and nxt.e == 0:
                        pe.wait_ge(pos_read, 2 * B)
                    transpose_x(nxt)
                if after(j.n, 1):
                    job_down(Job(g, i - 1))
                else:
                    shared_down_begin(B - 1)
                    down(w_odd, 1, 2)
                    shared_down_end(B - 1)
                job_hT(j)

            pe.wait_ge(wl13, 4)
            by_turns(pe, job)
            job_down(end)


def kernel(**inputs):
    import numpy as _np
    import concourse.bacc as _bacc
    from concourse import mybir as _mybir
    from concourse.bass_utils import run_bass_kernel_spmd as _run

    x = _np.ascontiguousarray(inputs["x"])
    ctx = _np.ascontiguousarray(inputs["ctx_2048"])
    mask = _np.ascontiguousarray(inputs["mask_BxS2_bk0"])
    gate_w, w1, w2, w3, sw1, sw2, sw3 = (
        _np.asarray(inputs["L0_ffn_" + n]) for n in ("gate_w", "w1", "w2", "w3", "sw1", "sw2", "sw3"))
    B, S, D = x.shape
    E, I, _ = w1.shape
    kd, n2 = D // 128, sw1.shape[0] // I
    a1 = _np.concatenate([sw1.reshape(n2, I, D), w1])
    a3 = _np.concatenate([sw3.reshape(n2, I, D), w3])
    a2 = _np.concatenate([sw2.reshape(D, n2, I).transpose(1, 0, 2), w2])
    w13 = _np.stack([a1, a3], axis=1).reshape(n2 + E, 2 * I, kd, 128).transpose(0, 3, 2, 1)
    a2 = a2.transpose(0, 2, 1)
    arrays = {
        "x": x,
        "ctx": ctx,
        "ctx_t": ctx.reshape(B, S, kd, 128).transpose(0, 3, 2, 1),
        "mask": mask,
        "gate_t": gate_w.reshape(E, kd, 128).transpose(2, 1, 0),
        "w13": w13,
        "w2ab": a2[:, 0:256].reshape(n2 + E, 2, 128, D).transpose(0, 2, 1, 3),
        "w2c": a2[:, 256:],
    }
    nc = _bacc.Bacc("TRN2", target_bir_lowering=False, num_devices=1)
    args, ins = [], {}
    for name, a in arrays.items():
        a = _np.ascontiguousarray(a)
        ins[f"in_{name}"] = a
        args.append(nc.dram_tensor(f"in_{name}", a.shape, _mybir.dt.from_np(a.dtype), kind="ExternalInput").ap())
    args.append(nc.dram_tensor("out_0", (B * S + 128, D), _mybir.dt.float32, kind="ExternalOutput").ap())
    cross_attention_moe_kernel(nc, *args)
    r = _run(nc, [ins], core_ids=[0])
    return r.results[0]["out_0"][:B * S].reshape(B, S, D)
```
